# Optimizing a Trainium2 kernel written in Bass

```python
import numpy as np
import jax
import jax.numpy as jnp

def _softmax(x, axis=-1):
    return jax.nn.softmax(x, axis=axis)

def _gelu(x):
    return jax.nn.gelu(x, approximate=True)

def _silu(x):
    return jax.nn.silu(x)

def _sigmoid(x):
    return jax.nn.sigmoid(x)

def _layernorm(x, axis=-1, eps=1e-05):
    m = jnp.mean(x, axis=axis, keepdims=True)
    v = jnp.var(x, axis=axis, keepdims=True)
    return (x - m) / jnp.sqrt(v + eps)

def _scatter_add(tgt, idx, src, axis=0):
    return tgt.at[idx].add(src)

def _segment_sum(src, seg, n):
    return jax.ops.segment_sum(src, seg, n)
kernel_name = 'mk_macaron_d1_jaxref_r4_e3b5d6'

def setup_inputs(seed: int=0):
    np.random.seed(seed)
    _w = jnp.asarray

    def _L0_attn_setup():
        import jax, jax.numpy as jnp
        import numpy as np
        DIM = 512
        H = 4
        KD = 512
        VD = 256
        DK = KD // H
        DV = VD // H
        LOW = 16
        NORMALIZER = 16.0
        EPS = 1e-05
        CHUNK = 64
        B, L = (2, 1024)

        def _chunk_gla(q, k, v, gk):
            b_, h_, l_, dk = q.shape
            dv = v.shape[-1]
            nc = l_ // CHUNK
            scale = dk ** (-0.5)

            def to_chunks(t):
                d = t.shape[-1]
                return t.reshape(b_, h_, nc, CHUNK, d).transpose(2, 0, 1, 3, 4)
            qc, kc, vc, gc = map(to_chunks, (q, k, v, gk))
            mask = jnp.tril(jnp.ones((CHUNK, CHUNK), bool))

            def step(S, inp):
                qi, ki, vi, gi = inp
                b = jnp.cumsum(gi, axis=-2)
                qe = qi * jnp.exp(b) * scale
                kd = ki * jnp.exp(-b)
                A = jnp.einsum('bhcd,bhsd->bhcs', qe, kd)
                A = jnp.where(mask, A, 0.0)
                o = jnp.einsum('bhcs,bhsv->bhcv', A, vi) + jnp.einsum('bhcd,bhdv->bhcv', qe, S)
                blast = b[..., -1:, :]
                S_new = jnp.exp(blast)[..., 0, :, None] * S + jnp.einsum('bhcd,bhcv->bhdv', ki * jnp.exp(blast - b), vi)
                return (S_new, o)
            S0 = jnp.zeros((b_, h_, dk, dv), q.dtype)
            _, outs = jax.lax.scan(step, S0, (qc, kc, vc, gc))
            return outs.transpose(1, 2, 0, 3, 4).reshape(b_, h_, l_, dv)
        key = jax.random.key(seed)
        ks = jax.random.split(key, 10)
        s = 0.02
        return {'x': jax.random.normal(ks[0], (B, L, DIM), jnp.float32), 'Wq': jax.random.normal(ks[1], (DIM, KD), jnp.float32) * s, 'Wk': jax.random.normal(ks[2], (DIM, KD), jnp.float32) * s, 'Wv': jax.random.normal(ks[3], (DIM, VD), jnp.float32) * s, 'Wgk1': jax.random.normal(ks[4], (DIM, LOW), jnp.float32) * s, 'Wgk2': jax.random.normal(ks[5], (LOW, KD), jnp.float32) * s, 'bgk2': jnp.zeros((KD,), jnp.float32), 'Wg': jax.random.normal(ks[6], (DIM, VD), jnp.float32) * s, 'Wnorm': jnp.ones((DV,), jnp.float32), 'Wo': jax.random.normal(ks[7], (VD, DIM), jnp.float32) * s}
    _L0_attn_in = _L0_attn_setup()

    def _L0_ffn_setup():
        import jax, jax.numpy as jnp
        import numpy as np
        TOP_K = 8
        NEG_INF = -1000000000.0
        key = jax.random.key(seed)
        ks = jax.random.split(key, 6)
        B, S, H, I, E, G, GS = (1, 512, 512, 352, 64, 8, 8)
        sc = 0.02
        return {'hidden_states': jax.random.normal(ks[0], (B, S, H), jnp.float32), 'gate_w': jax.random.normal(ks[1], (E, H), jnp.float32) * sc, 'mask_up_w': jax.random.normal(ks[2], (G, H, GS), jnp.float32) * sc, 'gate_proj_w': jax.random.normal(ks[3], (G, I, H), jnp.float32) * sc, 'up_proj_w': jax.random.normal(ks[4], (G, I, H), jnp.float32) * sc, 'down_proj_w': jax.random.normal(ks[5], (G, H, I), jnp.float32) * sc, 'inv_map': jnp.arange(G * GS, dtype=jnp.int64).reshape(G, GS)}
    _L0_ffn_in = _L0_ffn_setup()
    _d = {'L0_attn_x': _L0_attn_in['x'], 'L0_attn_Wq': _L0_attn_in['Wq'], 'L0_attn_Wk': _L0_attn_in['Wk'], 'L0_attn_Wv': _L0_attn_in['Wv'], 'L0_attn_Wgk1': _L0_attn_in['Wgk1'], 'L0_attn_Wgk2': _L0_attn_in['Wgk2'], 'L0_attn_bgk2': _L0_attn_in['bgk2'], 'L0_attn_Wg': _L0_attn_in['Wg'], 'L0_attn_Wnorm': _L0_attn_in['Wnorm'], 'L0_attn_Wo': _L0_attn_in['Wo'], 'L0_ffn_gate_w': _L0_ffn_in['gate_w'], 'L0_ffn_mask_up_w': _L0_ffn_in['mask_up_w'], 'L0_ffn_gate_proj_w': _L0_ffn_in['gate_proj_w'], 'L0_ffn_up_proj_w': _L0_ffn_in['up_proj_w'], 'L0_ffn_down_proj_w': _L0_ffn_in['down_proj_w'], 'L0_ffn_inv_map': _L0_ffn_in['inv_map']}
    _x0 = _d['L0_attn_x']
    _d['L0_attn_x'] = jax.random.normal(jax.random.fold_in(jax.random.key(seed), 1), (2, 1024, 512), dtype=_x0.dtype)
    del _x0
    return _d

def reference(L0_attn_x, L0_attn_Wq, L0_attn_Wk, L0_attn_Wv, L0_attn_Wgk1, L0_attn_Wgk2, L0_attn_bgk2, L0_attn_Wg, L0_attn_Wnorm, L0_attn_Wo, L0_ffn_gate_w, L0_ffn_mask_up_w, L0_ffn_gate_proj_w, L0_ffn_up_proj_w, L0_ffn_down_proj_w, L0_ffn_inv_map):

    def _L0_attn_ref(x, Wq, Wk, Wv, Wgk1, Wgk2, bgk2, Wg, Wnorm, Wo):
        import jax, jax.numpy as jnp
        import numpy as np
        DIM = 512
        H = 4
        KD = 512
        VD = 256
        DK = KD // H
        DV = VD // H
        LOW = 16
        NORMALIZER = 16.0
        EPS = 1e-05
        CHUNK = 64
        B, L = (2, 1024)

        def _chunk_gla(q, k, v, gk):
            b_, h_, l_, dk = q.shape
            dv = v.shape[-1]
            nc = l_ // CHUNK
            scale = dk ** (-0.5)

            def to_chunks(t):
                d = t.shape[-1]
                return t.reshape(b_, h_, nc, CHUNK, d).transpose(2, 0, 1, 3, 4)
            qc, kc, vc, gc = map(to_chunks, (q, k, v, gk))
            mask = jnp.tril(jnp.ones((CHUNK, CHUNK), bool))

            def step(S, inp):
                qi, ki, vi, gi = inp
                b = jnp.cumsum(gi, axis=-2)
                qe = qi * jnp.exp(b) * scale
                kd = ki * jnp.exp(-b)
                A = jnp.einsum('bhcd,bhsd->bhcs', qe, kd)
                A = jnp.where(mask, A, 0.0)
                o = jnp.einsum('bhcs,bhsv->bhcv', A, vi) + jnp.einsum('bhcd,bhdv->bhcv', qe, S)
                blast = b[..., -1:, :]
                S_new = jnp.exp(blast)[..., 0, :, None] * S + jnp.einsum('bhcd,bhcv->bhdv', ki * jnp.exp(blast - b), vi)
                return (S_new, o)
            S0 = jnp.zeros((b_, h_, dk, dv), q.dtype)
            _, outs = jax.lax.scan(step, S0, (qc, kc, vc, gc))
            return outs.transpose(1, 2, 0, 3, 4).reshape(b_, h_, l_, dv)
        b_, l_, _ = x.shape

        def heads(t, d):
            return t.reshape(b_, l_, H, d).transpose(0, 2, 1, 3)
        q = heads(x @ Wq, DK)
        k = heads(x @ Wk, DK)
        v = heads(x @ Wv, DV)
        gk = heads(x @ Wgk1 @ Wgk2 + bgk2, DK)
        gk = jax.nn.log_sigmoid(gk) / NORMALIZER
        o = _chunk_gla(q, k, v, gk)
        o = o.transpose(0, 2, 1, 3)
        g = (x @ Wg).reshape(b_, l_, H, DV)
        rms = o * jax.lax.rsqrt(jnp.mean(o * o, axis=-1, keepdims=True) + EPS) * Wnorm
        o = rms * (g * jax.nn.sigmoid(g))
        return o.reshape(b_, l_, VD) @ Wo

    def _L0_ffn_ref(hidden_states, gate_w, mask_up_w, gate_proj_w, up_proj_w, down_proj_w, inv_map):
        import jax, jax.numpy as jnp
        import numpy as np
        TOP_K = 8
        NEG_INF = -1000000000.0
        B, S, H = hidden_states.shape
        x = hidden_states.reshape(-1, H)
        N = x.shape[0]
        E = gate_w.shape[0]
        scores = jax.nn.softmax(x @ gate_w.T, axis=-1)
        topk_w, topk_idx = jax.lax.top_k(scores, TOP_K)
        w_e = jnp.zeros((N, E), x.dtype).at[jnp.arange(N)[:, None], topk_idx].add(topk_w)
        flat = w_e[:, inv_map]
        scalar = flat.sum(-1)
        soft = jax.nn.softmax(jnp.where(flat == 0, NEG_INF, flat), axis=-1)
        xg = x[:, None, :] + jnp.einsum('ngi,ghi->ngh', soft, mask_up_w)
        g = jnp.einsum('ngh,gih->ngi', xg, gate_proj_w)
        u = jnp.einsum('ngh,gih->ngi', xg, up_proj_w)
        a = jax.nn.silu(g) * u
        d = jnp.einsum('ngi,ghi->ngh', a, down_proj_w)
        y = jnp.einsum('ng,ngh->nh', scalar, d)
        return y.reshape(B, S, H)
    x = L0_attn_x
    x = x + 0.5 * _L0_ffn_ref(_layernorm(x, axis=-1), L0_ffn_gate_w, L0_ffn_mask_up_w, L0_ffn_gate_proj_w, L0_ffn_up_proj_w, L0_ffn_down_proj_w, L0_ffn_inv_map)
    x = x + _L0_attn_ref(_layernorm(x, axis=-1), L0_attn_Wq, L0_attn_Wk, L0_attn_Wv, L0_attn_Wgk1, L0_attn_Wgk2, L0_attn_bgk2, L0_attn_Wg, L0_attn_Wnorm, L0_attn_Wo)
    x = x + 0.5 * _L0_ffn_ref(_layernorm(x, axis=-1), L0_ffn_gate_w, L0_ffn_mask_up_w, L0_ffn_gate_proj_w, L0_ffn_up_proj_w, L0_ffn_down_proj_w, L0_ffn_inv_map)
    return x

_drawn_inputs = setup_inputs


def setup_inputs(seed=0):
    import zlib

    import numpy as np

    out = dict(_drawn_inputs(seed))
    spreads = {'L0_attn_bgk2': (0.0, 0.8), 'L0_attn_Wnorm': (1.0, 0.6)}
    factors = {'L0_attn_Wgk1': 8.0,
     'L0_attn_Wgk2': 8.0,
     'L0_ffn_gate_w': 8.0,
     'L0_ffn_mask_up_w': 8.0,
     'L0_ffn_gate_proj_w': 6.664,
     'L0_ffn_up_proj_w': 6.701,
     'L0_ffn_down_proj_w': 6.565}
    for name, (base, spread) in spreads.items():
        noise = np.random.default_rng([zlib.crc32(name.encode()), seed]).standard_normal(out[name].shape)
        drawn = base * np.exp(spread * noise) if base else spread * noise
        out[name] = jnp.asarray(drawn.astype(out[name].dtype))
    for name, factor in factors.items():
        out[name] = (out[name] * factor).astype(out[name].dtype)
    return out
```

```python
from contextlib import ExitStack

import numpy as np

import concourse.bass as bass
from concourse import mybir

ALU = mybir.AluOpType
ACT = mybir.ActivationFunctionType
AX = mybir.AxisListType
F32 = mybir.dt.float32
F32R = mybir.dt.float32r
I32 = mybir.dt.int32

P = 128
TOK = 2048
SEQ = 1024
D = 512
KC = D // P
NB = 512
BLOCKS = TOK // NB
BPS = SEQ // NB
NT = NB // P
E = 64
G = 8
GS = E // G
I = 352
HALF = G * I // 2 // P
CH = 2 * HALF
GW = 2 * P * KC
TOPK = 8
H = 4
DV = 64
LOW = 16
CK = 64
NCK = NB // CK
EPS = 1e-5
SCALE = float(P) ** -0.5
NORM = 1.0 / 16.0
CREDIT = 2

AT_SLABS = H + 2
GU_BLOCK = 2 * CH + AT_SLABS
GU_AT = CH
GU_F2 = CH + AT_SLABS
R_STEPS = 22
A_STEPS = 68


def build(nc, x, wgu, wdn, wat, w_gate, w_mup, w_gk1, w_gk2, bgk, wnorm, wo, inv, c_id, c_mask, c_reset, c_iota, out):
    with ExitStack() as ctx:
        def sb(name, shape, dt=F32):
            return ctx.enter_context(nc.sbuf_tensor(name, shape, dt))

        def sem(name):
            return ctx.enter_context(nc.semaphore(name))

        raw_gu = sb("raw_gu", [P, 2, GW])
        raw_d = sb("raw_d", [P, 2, D])
        gu_hi = sb("gu_hi", [P, 2, GW], F32R)
        gu_lo = sb("gu_lo", [P, 2, GW], F32R)
        d_hi = sb("d_hi", [P, 2, D], F32R)
        d_lo = sb("d_lo", [P, 2, D], F32R)
        x_in = sb("x_in", [P, NT, D])
        x_res = sb("x_res", [P, NT, D])
        xn = sb("xn", [P, NT, D])
        x_hi = sb("x_hi", [P, KC, NB], F32R)
        x_lo = sb("x_lo", [P, KC, NB], F32R)
        m_all = sb("m_all", [P, 2, HALF, 2 * P])
        mask = sb("mask", [P, HALF, P])
        m_st = sb("m_st", [P, 2, 2 * P], F32R)
        mask_st = sb("mask_st", [P, 2, P], F32R)
        softT = sb("softT", [P, 2, NB], F32R)
        flatT = sb("flatT", [P, NB], F32R)
        a_hi = sb("a_hi", [P, 2, NB], F32R)
        a_lo = sb("a_lo", [P, 2, NB], F32R)
        tmp = sb("tmp", [P, 6, NB])
        wo_hi = sb("wo_hi", [P, 2, D], F32R)
        wo_lo = sb("wo_lo", [P, 2, D], F32R)
        gate_s = sb("gate_s", [P, KC, 2 * E], F32R)
        k1_hi = sb("k1_hi", [P, KC, LOW], F32R)
        k1_lo = sb("k1_lo", [P, KC, LOW], F32R)
        mup_hi = sb("mup_hi", [P, 2, KC, P], F32R)
        mup_lo = sb("mup_lo", [P, 2, KC, P], F32R)
        gk2_s = sb("gk2_s", [LOW, D])
        bias = sb("bias", [P, H])
        wn = sb("wn", [P, DV])
        ident = sb("ident", [P, P])
        reset = sb("reset", [P, NB])
        perm = sb("perm", [E, E])
        perm_i = sb("perm_i", [E, E], I32)
        perm_w = sb("perm_w", [E, E])
        iota = sb("iota", [E, 1])
        stats = sb("stats", [P, NT, 6])
        mv = sb("mv", [P, NT, 2])
        ve = sb("ve", [P, NT])
        rstd = sb("rstd", [P, NT])
        mhalf = sb("mhalf", [P, 16])
        r_m = sb("r_m", [P, NT * G])
        r_s = sb("r_s", [P, NT * G])
        top = sb("top", [P, NT, TOPK])
        qe = sb("qe", [P, H, NB])
        k2 = sb("k2", [P, H, NB])
        k2t = sb("k2t", [P, H, NT, P])
        scm = sb("scm", [P, H, NT, P])
        vt = sb("vt", [P, NT, H * DV])
        gt = sb("gt", [P, NT, H * DV])
        dec = sb("dec", [P, H, NCK])
        state = sb("state", [P, NCK, H, DV])
        carry = sb("carry", [P, 2, H * DV])
        ms = sb("ms", [P, 16])
        rr = sb("rr", [P, 16])

        sig, t1, t2 = tmp[:, 0, :], tmp[:, 1, :], tmp[:, 2, :]
        m_raw, m_top = tmp[:, 3, 0:2 * P], tmp[:, 3, 2 * P:4 * P]
        route = tmp[:, 0:3, :].rearrange("p a b -> p (a b)").rearrange("p (t c) -> p t c", t=NT)
        w_eT = tmp[0:E, 3, :]
        kd = xn
        r_a, r_b, r_c = (k2[:, i, 0:NT * E].rearrange("p (t e) -> p t e", t=NT) for i in range(3))
        z1s = k2t[0:LOW, 0, :, :].rearrange("p t c -> p (t c)")
        o_sb = k2[:, 0:2, :].rearrange("p a b -> p (a b)")
        o_w = k2[:, 2:4, :].rearrange("p a b -> p (a b)")
        o_g = tmp[:, 0:2, :].rearrange("p a b -> p (a b)")
        og_hi, og_lo = a_hi, a_lo
        lsp, mn, bc, df, eb, enb = (tmp[:, i, :] for i in range(6))

        bank = [ctx.enter_context(nc.psum_tensor(f"bank{i}", [P, NB], F32)) for i in range(8)]
        YB, GB, UB, SB_, XB = bank[0:4], bank[4], bank[5], bank[6], bank[7]

        ld_const = sem("ld_const")
        ld_mup = sem("ld_mup")
        ld_x = sem("ld_x")
        st_out = sem("st_out")
        gu_in = [sem(f"gu_in{i}") for i in range(2)]
        d_in = [sem(f"d_in{i}") for i in range(2)]
        gu_hi_ok, gu_lo_ok = sem("gu_hi_ok"), sem("gu_lo_ok")
        d_hi_ok, d_lo_ok = sem("d_hi_ok"), sem("d_lo_ok")
        gu_used, d_used = sem("gu_used"), sem("d_used")
        pool_init, carry_zero = sem("pool_init"), sem("carry_zero")
        setup_hi, setup_lo = sem("setup_hi"), sem("setup_lo")
        perm_ok = sem("perm_ok")
        stats_ok, mv_ok, rstd_ok, xn_ok = sem("stats_ok"), sem("mv_ok"), sem("rstd_ok"), sem("xn_ok")
        ve_ok = sem("ve_ok")
        xT_ok, x_hi_ok, x_lo_ok = sem("xT_ok"), sem("x_hi_ok"), sem("x_lo_ok")
        logit_ok, logit_cp, exp_ok, wT_ok, wT_cp, flat_ok, sexp_ok, routeT_ok, route_cp = (
            sem(n) for n in ("logit_ok", "logit_cp", "exp_ok", "wT_ok", "wT_cp", "flat_ok", "sexp_ok", "routeT_ok", "route_cp"))
        rstep = sem("rstep")
        m_mm, m_masked, m_top_ok, m_ok, staged = (sem(n) for n in ("m_mm", "m_masked", "m_top_ok", "m_ok", "staged"))
        g_ok, u_ok, sig_e, sig_1, sig_r, g_free, gu_prod, us_free, a_hi_ok, a_lo_ok = (
            sem(n) for n in ("g_ok", "u_ok", "sig_e", "sig_1", "sig_r", "g_free", "gu_prod", "us_free", "a_hi_ok", "a_lo_ok"))
        x_ok = sem("x_ok")
        z1_ok, z1_cp, z_ok, q_ok, lsp_a, lsp_e, lsp_ok, eb_ok, enb_ok, ed_ok = (
            sem(n) for n in ("z1_ok", "z1_cp", "z_ok", "q_ok", "lsp_a", "lsp_e", "lsp_ok", "eb_ok", "enb_ok", "ed_ok"))
        astep = sem("astep")
        vg_ok, v_cp, k2T_ok, k2_cp, sc_ok, sc_cp, sc_mask, upd_ok, o_ok, o_cp, rms_v, rms_ok, sg_ok = (
            sem(n) for n in ("vg_ok", "v_cp", "k2T_ok", "k2_cp", "sc_ok", "sc_cp", "sc_mask", "upd_ok", "o_ok", "o_cp", "rms_v", "rms_ok", "sg_ok"))
        waited = sem("waited")
        ogT_ok, og_hi_ok, og_lo_ok, wo_ok = (sem(n) for n in ("ogT_ok", "og_hi_ok", "og_lo_ok", "wo_ok"))

        x_t = x.rearrange("(b t p) d -> b p t d", p=P, t=NT)
        out_t = out.rearrange("(b t p) d -> b p t d", p=P, t=NT)
        N_CONST = 10

        def wait(eng, s, v):
            if not (isinstance(v, int) and v <= 0):
                eng.wait_ge(s, v)

        def mup_copies(half):
            m = k2[:, 1, 0:KC * E].rearrange("p (k h e) -> p k h e", k=KC, h=2)[:, :, half, :]
            return m.unsqueeze(2).broadcast_to([P, KC, 4, E // 2])

        def update(h, c):
            col = (h % 2) * NB // 2 + (c // 2) * DV
            return ((GB, UB), (SB_, XB))[h // 2][c % 2][:, col:col + DV]

        def settled(eng):
            eng.sem_inc(waited, 1)

        def gu_at(t, off, i):
            return t * GU_BLOCK + off + i

        block = ctx.enter_context(nc.Block())

        @block.sync
        def _(sp):
            def slab(t, off, i, half, src):
                sp.wait_ge(gu_lo_ok, gu_at(t, off, i) + 1)
                sp.dma_start(raw_gu[:, half, :], src).then_inc(gu_in[half], 16)

            def dslab(n, half, src):
                sp.wait_ge(d_lo_ok, n + 1)
                sp.dma_start(raw_d[:, half, :], src).then_inc(d_in[half], 16)

            def ffn(t, ph):
                off = GU_F2 if ph else 0
                with sp.Fori(0, HALF) as j:
                    for half in range(2):
                        slab(t, off, j * 2 + half, half, wgu[half, j])
                        dslab((t * 2 + ph) * CH + j * 2 + half, half, wdn[half, j])

            def attn(t):
                for s in range(AT_SLABS):
                    slab(t, GU_AT, s, s % 2, wat[s])

            def blk(t, more):
                ffn(t, 0)
                attn(t)
                if more:
                    sp.wait_ge(x_ok, t * 3 + 1)
                    sp.dma_start(x_in[:], x_t[t + 1]).then_inc(ld_x, 16)
                ffn(t, 1)

            sp.dma_start(x_in[:], x_t[0]).then_inc(ld_x, 16)
            sp.dma_start(ident[:], c_id).then_inc(ld_const, 16)
            sp.dma_start(mask[:].rearrange("p a b -> p (a b)"), c_mask).then_inc(ld_const, 16)
            sp.dma_start(reset[:], c_reset).then_inc(ld_const, 16)
            sp.dma_start(iota[:], c_iota).then_inc(ld_const, 16)
            sp.dma_start(gk2_s[:], w_gk2).then_inc(ld_const, 16)
            sp.dma_start(bias[:], bgk).then_inc(ld_const, 16)
            sp.dma_start(wn[:], wnorm.partition_broadcast(P)).then_inc(ld_const, 16)
            sp.dma_start(perm_i[:], inv.partition_broadcast(E)).then_inc(ld_const, 16)
            sp.dma_start(k2[:, 0, :].rearrange("p (k e) -> p k e", k=KC)[:, :, 0:E], w_gate).then_inc(ld_const, 16)
            sp.dma_start(k2[:, 0, :].rearrange("p (k e) -> p k e", k=KC)[:, :, E:E + LOW], w_gk1).then_inc(ld_const, 16)
            sp.dma_start(k2[:, 1, 0:KC * E].rearrange("p (k e) -> p k e", k=KC), w_mup).then_inc(ld_mup, 16)
            sp.dma_start(k2[:, 2:4, :], wo).then_inc(ld_mup, 16)
            blk(0, True)
            with sp.Fori(1, BLOCKS - 1) as t:
                blk(t, True)
            blk(BLOCKS - 1, False)

        @block.gpsimd
        def _(pool):
            nc.gpsimd.memset(mhalf[:], -0.5).then_inc(pool_init, 1)
            nc.gpsimd.memset(carry[:], 0.0).then_inc(carry_zero, 1)
            nc.gpsimd.memset(scm[:], 0.0).then_inc(pool_init, 1)

            def rstd_of(r):
                pool.wait_ge(mv_ok, r + 1)
                settled(pool)
                nc.gpsimd.tensor_scalar(ve[:], mv[:, :, 1], EPS, None, ALU.add).then_inc(ve_ok, 1)
                pool.wait_ge(ve_ok, r + 1)
                nc.gpsimd.tensor_tensor(rstd[:], ve[:], mhalf[:, 0:NT], ALU.pow).then_inc(rstd_ok, 1)

            def ffn(t, ph, first):
                off = GU_F2 if ph else 0
                n0 = (t * 2 + ph) * CH
                rstd_of(t * 3 + 2 * ph)
                with pool.Fori(0, HALF) as j:
                    for half in range(2):
                        pool.wait_ge(gu_used, gu_at(t, off, j * 2 + half) + 1)
                        if first:
                            pool.wait_ge(m_ok, j * 2 + half + 1)
                        nc.gpsimd.tensor_copy(m_st[:, half, :], m_all[:, half, j, :])
                        nc.gpsimd.tensor_copy(mask_st[:, half, :], mask[:, j, :]).then_inc(staged, 1)

            def attn(t):
                rstd_of(t * 3 + 1)
                for h in range(H):
                    pool.wait_ge(sc_cp, t * H + h + 1)
                    settled(pool)
                    nc.gpsimd.affine_select(out=scm[:, h, :, :], in_=scm[:, h, :, :], compare_op=ALU.is_ge, fill=0.0,
                                            base=0, pattern=[[0, NT], [1, P]], channel_multiplier=-1).then_inc(sc_mask, 1)
                pool.wait_ge(rms_v, t * 2 + 2)
                nc.gpsimd.tensor_tensor(rr[:], ms[:], mhalf[:], ALU.pow).then_inc(rms_ok, 1)

            def blk(t, first):
                ffn(t, 0, first)
                attn(t)
                ffn(t, 1, False)
                pool.wait_ge(x_ok, t * 3 + 3)
                pool.dma_start(out_t[t], x_res[:]).then_inc(st_out, 16)

            pool.wait_ge(ld_const, 16 * N_CONST)
            blk(0, True)
            with pool.Fori(1, BLOCKS) as t:
                blk(t, False)
            pool.wait_ge(st_out, 16 * BLOCKS)

        @block.scalar
        def _(act):
            def copy(dst, src):
                return nc.scalar.activation(dst, src, ACT.Copy)

            def gu(t, off, j, half):
                act.wait_ge(gu_in[half], (t * (GU_BLOCK // 2) + off // 2 + j + 1) * 16)
                act.wait_ge(gu_used, gu_at(t, off, j * 2 + half) + 1)
                copy(gu_hi[:, half, :], raw_gu[:, half, :]).then_inc(gu_hi_ok, 1)

            def dn(t, ph, j, half):
                n = (t * 2 + ph) * CH + j * 2 + half
                act.wait_ge(d_in[half], ((t * 2 + ph) * HALF + j + 1) * 16)
                act.wait_ge(d_used, n + 1)
                copy(d_hi[:, half, :], raw_d[:, half, :]).then_inc(d_hi_ok, 1)

            def ln(r):
                for i in range(NT):
                    act.wait_ge(xT_ok, r * NT + i + 1)
                    copy(x_hi[:, :, i * P:(i + 1) * P], YB[i][:].rearrange("p (k c) -> p k c", k=KC)).then_inc(x_hi_ok, 1)

            def router(p):
                act.wait_ge(logit_ok, p + 1)
                copy(r_a[:], XB[:].rearrange("p (t c) -> p t c", t=NT)[:, :, 0:E]).then_inc(logit_cp, 1)
                act.wait_ge(rstep, p * R_STEPS + 3)
                nc.scalar.activation(r_b[:], r_b[:], ACT.Exp).then_inc(exp_ok, 1)
                act.wait_ge(wT_ok, p + 1)
                copy(w_eT, GB[0:E, :]).then_inc(wT_cp, 1)
                act.wait_ge(rstep, p * R_STEPS + 14)
                nc.scalar.activation(r_b[:], r_b[:], ACT.Exp).then_inc(sexp_ok, 1)
                for i in range(3):
                    act.wait_ge(routeT_ok, p * 3 + i + 1)
                    dst = softT[:, i, :] if i < 2 else flatT[:]
                    copy(dst, YB[i][:]).then_inc(route_cp, 1)

            def chunk(t, ph, j, half, last, first):
                off = GU_F2 if ph else 0
                n = (t * 2 + ph) * CH + j * 2 + half
                if half == 0:
                    gu(t, off, j, 1)
                elif not last:
                    gu(t, off, j + 1, 0)
                dn(t, ph, j, half)
                if first:
                    act.wait_ge(m_masked, n + 1)
                    copy(m_top.bitcast(F32R), m_raw).then_inc(m_top_ok, 1)
                act.wait_ge(g_ok, n + 1)
                nc.scalar.activation(sig, GB[:], ACT.Exp, scale=-1.0).then_inc(sig_e, 1)
                act.wait_ge(us_free, n + 1)
                act.wait_ge(d_used, n + 1)
                copy(a_hi[:, half, :], t2).then_inc(a_hi_ok, 1)

            def ffn(t, ph, first):
                ln(t * 3 + 2 * ph)
                router(t * 2 + ph)
                gu(t, GU_F2 if ph else 0, 0, 0)
                with act.Fori(0, HALF - 1) as j:
                    for half in range(2):
                        chunk(t, ph, j, half, False, first)
                for half in range(2):
                    chunk(t, ph, HALF - 1, half, True, first)

            def attn(t):
                ln(t * 3 + 1)
                act.wait_ge(z1_ok, t + 1)
                copy(z1s[:], XB[0:LOW, :]).then_inc(z1_cp, 1)
                for h in range(H):
                    gu(t, GU_AT, h // 2, h % 2)
                    act.wait_ge(astep, t * A_STEPS + 7 * h + 1)
                    nc.scalar.activation(lsp, YB[h % 2][:], ACT.Abs, bias=bias[:, h:h + 1]).then_inc(lsp_a, 1)
                    act.wait_ge(lsp_a, t * H + h + 1)
                    nc.scalar.activation(lsp, lsp, ACT.Exp, scale=-1.0).then_inc(lsp_e, 1)
                    act.wait_ge(lsp_e, t * H + h + 1)
                    nc.scalar.activation(lsp, lsp, ACT.Ln, bias=1.0).then_inc(lsp_ok, 1)
                    act.wait_ge(astep, t * A_STEPS + 7 * h + 3)
                    nc.scalar.activation(eb, bc, ACT.Exp, scale=NORM).then_inc(eb_ok, 1)
                    nc.scalar.activation(enb, bc, ACT.Exp, scale=-NORM).then_inc(enb_ok, 1)
                    act.wait_ge(astep, t * A_STEPS + 7 * h + 4)
                    nc.scalar.activation(df, df, ACT.Exp, scale=NORM).then_inc(ed_ok, 1)
                for s in range(2):
                    gu(t, GU_AT, H // 2, s)
                for i in range(NT):
                    if i < NT - 1:
                        act.wait_ge(vg_ok, t * (NT - 1) + i + 1)
                    else:
                        act.wait_ge(gu_used, gu_at(t, GU_AT, AT_SLABS) + CREDIT)
                    b = (SB_, XB)[i % 2]
                    copy(vt[:, i, :], b[:, 0:H * DV])
                    copy(gt[:, i, :], b[:, H * DV:]).then_inc(v_cp, 1)
                for h in range(H):
                    act.wait_ge(k2T_ok, t * H + h + 1)
                    copy(k2t[:, h, :, :], YB[h % 2][:].rearrange("p (t c) -> p t c", t=NT)).then_inc(k2_cp, 1)
                    act.wait_ge(sc_ok, t * H + h + 1)
                    if h == 0:
                        act.wait_ge(pool_init, 2)
                    b = YB[2 + h % 2][:].rearrange("p (t c) -> p t c", t=NT)
                    copy(scm[0:CK, h, :, 0:CK], b[0:CK, :, 0:CK])
                    copy(scm[CK:P, h, :, CK:P], b[CK:P, :, CK:P]).then_inc(sc_cp, 1)
                nc.scalar.activation(o_g, gt[:].rearrange("p t c -> p (t c)"), ACT.Exp, scale=-1.0).then_inc(sg_ok, 1)
                for i in range(2):
                    act.wait_ge(o_ok, t * 2 + i + 1)
                    copy(o_sb[:, i * NB:(i + 1) * NB], (SB_, XB)[i][:]).then_inc(o_cp, 1)
                for i in range(2):
                    act.wait_ge(ogT_ok, t * 2 + i + 1)
                    copy(og_hi[:, i, :], YB[i][:]).then_inc(og_hi_ok, 1)

            def blk(t, first):
                ffn(t, 0, first)
                attn(t)
                ffn(t, 1, False)

            act.wait_ge(ld_const, 16 * N_CONST)
            raw = k2[:, 0, :].rearrange("p (k e) -> p k e", k=KC)
            copy(gate_s[:, :, 0:E], raw[:, :, 0:E])
            copy(k1_hi[:], raw[:, :, E:E + LOW])
            act.wait_ge(ld_mup, 32)
            for half in range(2):
                copy(mup_hi[:, half, :, :].rearrange("p k (r e) -> p k r e", r=4), mup_copies(half))
            copy(wo_hi[:], k2[:, 2:4, :]).then_inc(setup_hi, 1)
            blk(0, True)
            with act.Fori(1, BLOCKS) as t:
                blk(t, False)

        @block.vector
        def _(dve):
            def tt(dst, a, b, op):
                return nc.vector.tensor_tensor(dst, a, b, op)

            def gu(t, off, j, half):
                dve.wait_ge(gu_hi_ok, gu_at(t, off, j * 2 + half) + 1)
                tt(gu_lo[:, half, :], raw_gu[:, half, :], gu_hi[:, half, :].bitcast(F32), ALU.subtract).then_inc(gu_lo_ok, 1)

            def dn(t, ph, j, half):
                dve.wait_ge(d_hi_ok, (t * 2 + ph) * CH + j * 2 + half + 1)
                tt(d_lo[:, half, :], raw_d[:, half, :], d_hi[:, half, :].bitcast(F32), ALU.subtract).then_inc(d_lo_ok, 1)

            def ln(r, src, t):
                if src is x_in:
                    dve.wait_ge(ld_x, (t + 1) * 16)
                for i in range(NT):
                    last = nc.vector.bn_stats(stats[:, i, :], src[:, i, :])
                last.then_inc(stats_ok, 1)
                dve.wait_ge(stats_ok, r + 1)
                settled(dve)
                for i in range(NT):
                    last = nc.vector.bn_aggr(mv[:, i, :], stats[:, i, :])
                last.then_inc(mv_ok, 1)
                dve.wait_ge(mv_ok, r + 1)
                dve.wait_ge(rstd_ok, r + 1)
                for i in range(NT):
                    nc.vector.tensor_scalar(xn[:, i, :], src[:, i, :], mv[:, i, 0:1], rstd[:, i:i + 1],
                                            ALU.subtract, ALU.mult).then_inc(xn_ok, 1)
                for i in range(NT):
                    dve.wait_ge(x_hi_ok, r * NT + i + 1)
                    tt(x_lo[:, :, i * P:(i + 1) * P], YB[i][:].rearrange("p (k c) -> p k c", k=KC),
                       x_hi[:, :, i * P:(i + 1) * P].bitcast(F32), ALU.subtract).then_inc(x_lo_ok, 1)

            def chain(s, base):
                n = [0]

                def step(ins, alone=False):
                    n[0] += 1
                    ins.then_inc(s, 1)
                    dve.wait_ge(s, base + n[0])
                    if alone:
                        settled(dve)
                return step, n

            def bcast(ap, n):
                return ap.unsqueeze(len(ap.shape)).broadcast_to(list(ap.shape) + [n])

            def router(p):
                step, n = chain(rstep, p * R_STEPS)
                r_g = [v[:].rearrange("p t (g s) -> p (t g) s", g=G) for v in (r_a, r_b, r_c)]
                mx, sm = r_m[:, 0:NT], r_s[:, 0:NT]
                dve.wait_ge(logit_cp, p + 1)
                step(tt(r_a[:], XB[:].rearrange("p (t c) -> p t c", t=NT)[:, :, E:2 * E], r_a[:], ALU.add))
                step(nc.vector.tensor_reduce(mx, r_a[:], AX.X, ALU.max))
                step(tt(r_b[:], r_a[:], bcast(mx, E), ALU.subtract))
                dve.wait_ge(exp_ok, p + 1)
                step(nc.vector.tensor_reduce(sm, r_b[:], AX.X, ALU.add))
                step(nc.vector.reciprocal(sm, sm))
                step(tt(r_a[:], r_b[:], bcast(sm, E), ALU.mult), True)
                for i in range(NT):
                    last = nc.vector.max(top[:, i, :], r_a[:, i, :])
                step(last, True)
                for i in range(NT):
                    last = nc.vector.match_replace(r_b[:, i, :], top[:, i, :], r_a[:, i, :], 0.0)
                step(last)
                step(tt(r_c[:], r_a[:], r_b[:], ALU.subtract))
                dve.wait_ge(flat_ok, p + 1)
                step(nc.vector.tensor_copy(r_c[:], UB[:, 0:NT * E].rearrange("p (t e) -> p t e", t=NT)))
                step(nc.vector.tensor_scalar(r_a[:], r_c[:], 0.0, -1e9, ALU.is_equal, ALU.mult))
                step(tt(r_a[:], r_a[:], r_c[:], ALU.add))
                step(nc.vector.tensor_reduce(r_m[:], r_g[0], AX.X, ALU.max))
                step(tt(r_g[1], r_g[0], bcast(r_m[:], GS), ALU.subtract))
                dve.wait_ge(sexp_ok, p + 1)
                step(nc.vector.tensor_reduce(r_s[:], r_g[1], AX.X, ALU.add))
                step(nc.vector.reciprocal(r_s[:], r_s[:]))
                step(tt(r_g[0], r_g[1], bcast(r_s[:], GS), ALU.mult))
                HE = E // 2
                soft = r_a[:].rearrange("p t (h e) -> p t h e", h=2)
                flat = r_c[:].rearrange("p t (h e) -> p t h e", h=2)
                rs = route[:, :, 0:2 * P].rearrange("p t (h c) -> p t h c", h=2)
                rf = route[:, :, 2 * P:3 * P].rearrange("p t (h c) -> p t h c", h=2)
                step(nc.vector.tensor_copy(rs[:, :, :, 0:HE].bitcast(F32R), soft))
                step(tt(rs[:, :, :, HE:2 * HE], soft, rs[:, :, :, 0:HE], ALU.subtract))
                step(nc.vector.tensor_copy(rs[:, :, :, 2 * HE:4 * HE], rs[:, :, :, 0:2 * HE]))
                step(nc.vector.tensor_copy(rf[:, :, :, 0:HE].bitcast(F32R), flat))
                step(tt(rf[:, :, :, HE:2 * HE], flat, rf[:, :, :, 0:HE], ALU.subtract))
                assert n[0] == R_STEPS, n

            def chunk(t, ph, j, half, last, first):
                off = GU_F2 if ph else 0
                n = (t * 2 + ph) * CH + j * 2 + half
                if half == 0:
                    gu(t, off, j, 1)
                elif not last:
                    gu(t, off, j + 1, 0)
                dn(t, ph, j, half)
                if first:
                    dve.wait_ge(m_mm, n + 1)
                    mb = mask[:, j, :].unsqueeze(1).broadcast_to([P, 2, P])
                    tt(m_raw.rearrange("p (a c) -> p a c", a=2), XB[:, 0:2 * P].rearrange("p (a c) -> p a c", a=2),
                       mb, ALU.mult).then_inc(m_masked, 1)
                    dve.wait_ge(m_top_ok, n + 1)
                    nc.vector.tensor_copy(m_all[0:E, half, j, :], m_top[0:E, :])
                    tt(m_all[E:P, half, j, :], m_raw[E:P, :], m_top[E:P, :], ALU.subtract).then_inc(m_ok, 1)
                dve.wait_ge(sig_e, n + 1)
                nc.vector.tensor_scalar(sig, sig, 1.0, None, ALU.add).then_inc(sig_1, 1)
                dve.wait_ge(sig_1, n + 1)
                nc.vector.reciprocal(sig, sig).then_inc(sig_r, 1)
                dve.wait_ge(sig_r, n + 1)
                tt(t1, GB[:], sig, ALU.mult).then_inc(g_free, 1)
                dve.wait_ge(g_free, n + 1)
                dve.wait_ge(u_ok, n + 1)
                tt(t1, UB[:], t1, ALU.mult).then_inc(gu_prod, 1)
                dve.wait_ge(gu_prod, n + 1)
                dve.wait_ge(gu_used, gu_at(t, off, j * 2 + half) + 1 + CREDIT)
                tt(t2, SB_[:], t1, ALU.mult).then_inc(us_free, 1)
                dve.wait_ge(us_free, n + 1)
                dve.wait_ge(a_hi_ok, n + 1)
                tt(a_lo[:, half, :], t2, a_hi[:, half, :].bitcast(F32), ALU.subtract).then_inc(a_lo_ok, 1)

            def ffn(t, ph, first):
                src = x_res if ph else x_in
                ln(t * 3 + 2 * ph, src, t)
                router(t * 2 + ph)
                gu(t, GU_F2 if ph else 0, 0, 0)
                with dve.Fori(0, HALF - 1) as j:
                    for half in range(2):
                        chunk(t, ph, j, half, False, first)
                for half in range(2):
                    chunk(t, ph, HALF - 1, half, True, first)
                dve.wait_ge(d_used, (t * 2 + ph + 1) * CH + CREDIT)
                if not ph:
                    wait(dve, st_out, t * 16)
                for i in range(NT):
                    last = nc.vector.scalar_tensor_tensor(x_res[:, i, :], YB[i][:], 0.5, src[:, i, :], ALU.mult, ALU.add)
                last.then_inc(x_ok, 1)
                dve.wait_ge(x_ok, t * 3 + 2 * ph + 1)

            def attn(t):
                ln(t * 3 + 1, x_res, t)
                step, n = chain(astep, t * A_STEPS)
                for h in range(H):
                    gu(t, GU_AT, h // 2, h % 2)
                    dve.wait_ge(z_ok, t * H + h + 1)
                    step(nc.vector.tensor_scalar(mn, YB[h % 2][:], bias[:, h:h + 1], 0.0, ALU.add, ALU.min))
                    dve.wait_ge(lsp_ok, t * H + h + 1)
                    step(tt(mn, mn, lsp, ALU.subtract))
                    step(nc.vector.tensor_tensor_scan(bc, reset[:], mn, 0.0, ALU.mult, ALU.add))
                    b3 = bc.rearrange("p (c s) -> p c s", s=CK)
                    step(tt(df.rearrange("p (c s) -> p c s", s=CK), b3[:, :, CK - 1:CK].broadcast_to([P, NCK, CK]), b3, ALU.subtract))
                    dve.wait_ge(q_ok, t * H + h + 1)
                    dve.wait_ge(eb_ok, t * H + h + 1)
                    nc.vector.scalar_tensor_tensor(qe[:, h, :], YB[2 + h % 2][:], SCALE, eb, ALU.mult, ALU.mult)
                    step(nc.vector.tensor_copy(dec[:, h, :], eb.rearrange("p (c s) -> p c s", s=CK)[:, :, CK - 1]))
                    dve.wait_ge(gu_used, gu_at(t, GU_AT, h) + 1 + CREDIT)
                    dve.wait_ge(enb_ok, t * H + h + 1)
                    kb = (GB, UB)[h % 2]
                    step(tt(kd[:, h, :], kb[:], enb, ALU.mult))
                    dve.wait_ge(ed_ok, t * H + h + 1)
                    step(tt(k2[:, h, :], kb[:], df, ALU.mult))
                for s in range(2):
                    gu(t, GU_AT, H // 2, s)
                if isinstance(t, int):
                    slot = carry[:, t % BPS, :]
                    dve.wait_ge(carry_zero, 1)
                else:
                    slot = carry[:, t % BPS, :]
                step(nc.vector.tensor_copy(state[:, 0, :, :].rearrange("p h v -> p (h v)"), slot))
                for h in range(H):
                    dve.wait_ge(upd_ok, t * H + h // 2 * 2 + 2)
                    for c in range(NCK):
                        new = state[:, c + 1, h, :] if c + 1 < NCK else carry[:, 1, h * DV:(h + 1) * DV]
                        step(nc.vector.scalar_tensor_tensor(new, state[:, c, h, :], dec[:, h, c:c + 1],
                                                            update(h, c), ALU.mult, ALU.add))
                o3, w3 = (v.rearrange("p (a v) -> p a v", v=DV) for v in (o_sb, o_w))
                g1 = gt[:].rearrange("p t c -> p (t c)")
                dve.wait_ge(sg_ok, t + 1)
                step(nc.vector.tensor_scalar(o_g, o_g, 1.0, None, ALU.add))
                step(nc.vector.reciprocal(o_g, o_g))
                step(tt(o_g, o_g, g1, ALU.mult))
                step(tt(o_g.rearrange("p (a v) -> p a v", v=DV), o_g.rearrange("p (a v) -> p a v", v=DV),
                        wn[:].unsqueeze(1).broadcast_to([P, 16, DV]), ALU.mult))
                dve.wait_ge(o_cp, t * 2 + 2)
                step(tt(o_w, o_sb, o_sb, ALU.mult))
                nc.vector.tensor_reduce(ms[:], w3, AX.X, ALU.add).then_inc(rms_v, 1)
                dve.wait_ge(rms_v, t * 2 + 1)
                nc.vector.tensor_scalar(ms[:], ms[:], 1.0 / DV, EPS, ALU.mult, ALU.add).then_inc(rms_v, 1)
                dve.wait_ge(rms_ok, t + 1)
                step(tt(w3, o3, bcast(rr[:], DV), ALU.mult))
                step(tt(o_w, o_w, o_g, ALU.mult))
                for i in range(2):
                    dve.wait_ge(og_hi_ok, t * 2 + i + 1)
                    tt(og_lo[:, i, :], YB[i][:], og_hi[:, i, :].bitcast(F32), ALU.subtract).then_inc(og_lo_ok, 1)
                for i in range(NT):
                    dve.wait_ge(wo_ok, t * NT + i + 1)
                    last = tt(x_res[:, i, :], (YB[2], YB[3], GB, UB)[i][:], x_res[:, i, :], ALU.add)
                last.then_inc(x_ok, 1)
                dve.wait_ge(x_ok, t * 3 + 2)
                assert n[0] == A_STEPS, n

            def blk(t, first):
                ffn(t, 0, first)
                attn(t)
                ffn(t, 1, False)

            dve.sem_inc(gu_lo_ok, CREDIT)
            dve.sem_inc(d_lo_ok, CREDIT)
            dve.wait_ge(ld_const, 16 * N_CONST)
            nc.vector.tensor_copy(perm_w[:], perm_i[:]).then_inc(perm_ok, 1)
            dve.wait_ge(perm_ok, 1)
            nc.vector.tensor_scalar(perm[:], perm_w[:], 0.0, float(E), ALU.is_lt, ALU.mult).then_inc(perm_ok, 1)
            dve.wait_ge(perm_ok, 2)
            tt(perm[:], perm[:], perm_w[:], ALU.add).then_inc(perm_ok, 1)
            dve.wait_ge(perm_ok, 3)
            nc.vector.tensor_scalar(perm[:], perm[:], iota[:, 0:1], None, ALU.is_equal).then_inc(perm_ok, 1)
            dve.wait_ge(setup_hi, 1)
            raw = k2[:, 0, :].rearrange("p (k e) -> p k e", k=KC)
            tt(gate_s[:, :, E:2 * E], raw[:, :, 0:E], gate_s[:, :, 0:E].bitcast(F32), ALU.subtract)
            tt(k1_lo[:], raw[:, :, E:E + LOW], k1_hi[:].bitcast(F32), ALU.subtract)
            for half in range(2):
                tt(mup_lo[:, half, :, :].rearrange("p k (r e) -> p k r e", r=4), mup_copies(half),
                   mup_hi[:, half, :, :].bitcast(F32).rearrange("p k (r e) -> p k r e", r=4), ALU.subtract)
            tt(wo_lo[:], k2[:, 2:4, :], wo_hi[:].bitcast(F32), ALU.subtract).then_inc(setup_lo, 1)
            blk(0, True)
            with dve.Fori(1, BLOCKS) as t:
                blk(t, False)

        @block.tensor
        def _(pe):
            mm = nc.tensor.matmul

            def three(dst, w, xs, start, stop):
                (wh, wl), (xh, xl) = w, xs
                mm(dst, wh, xh, start=start, stop=False)
                mm(dst, wl, xh, start=False, stop=False)
                return mm(dst, wh, xl, start=False, stop=stop)

            def ln(r):
                for i in range(NT):
                    pe.wait_ge(xn_ok, r * NT + i + 1)
                    for k in range(KC):
                        last = nc.tensor.transpose(YB[i][:, k * P:(k + 1) * P], xn[:, i, k * P:(k + 1) * P], ident[:])
                    last.then_inc(xT_ok, 1)

            def router(r, p):
                for i in range(NT):
                    pe.wait_ge(x_lo_ok, r * NT + i + 1)
                    for k in range(KC):
                        for part in (x_hi, x_lo):
                            last = mm(XB[:, i * P:(i + 1) * P], part[:, k, i * P:(i + 1) * P], gate_s[:, k, :],
                                      start=(k == 0 and part is x_hi), stop=(k == KC - 1 and part is x_lo))
                last.then_inc(logit_ok, 1)
                pe.wait_ge(rstep, p * R_STEPS + 9)
                settled(pe)
                for i in range(NT):
                    last = nc.tensor.transpose(GB[0:E, i * P:(i + 1) * P], r_c[:, i, :], ident[:])
                last.then_inc(wT_ok, 1)
                pe.wait_ge(wT_cp, p + 1)
                for i in range(NT):
                    last = mm(UB[:, i * E:(i + 1) * E], w_eT[:, i * P:(i + 1) * P], perm[:], start=True, stop=True)
                last.then_inc(flat_ok, 1)
                pe.wait_ge(rstep, p * R_STEPS + R_STEPS)
                for s in range(3):
                    for i in range(NT):
                        last = nc.tensor.transpose(YB[s][:, i * P:(i + 1) * P], route[:, i, s * P:(s + 1) * P], ident[:])
                    last.then_inc(routeT_ok, 1)

            def xk(k):
                return x_hi[:, k, :], x_lo[:, k, :]

            def gu(t, ph, j, half, first):
                off = GU_F2 if ph else 0
                n = (t * 2 + ph) * CH + j * 2 + half
                pe.wait_ge(gu_lo_ok, gu_at(t, off, j * 2 + half) + 1 + CREDIT)
                hi, lo = (v[:, half, :].rearrange("p (k c) -> p k c", k=KC) for v in (gu_hi, gu_lo))
                if first:
                    wait(pe, m_masked, n)
                    for k in range(KC):
                        mm(XB[:, 0:2 * P], mup_hi[:, half, k, :], hi[:, k, :], start=(k == 0), stop=False)
                        mm(XB[:, 0:2 * P], mup_lo[:, half, k, :], hi[:, k, :], start=False, stop=False)
                        mm(XB[:, 0:2 * P], mup_hi[:, half, k, :], lo[:, k, :], start=False, stop=False)
                        last = mm(XB[:, 0:2 * P], mup_lo[:, half, k, :], lo[:, k, :], start=False, stop=(k == KC - 1))
                    last.then_inc(m_mm, 1)

                def main(b, c):
                    for k in range(KC):
                        three(b[:], (hi[:, k, c:c + P], lo[:, k, c:c + P]), xk(k), k == 0, False)

                def soft(b, c):
                    return mm(b[:], m_st[:, half, c:c + P], softT[:, half, :], start=False, stop=True)

                wait(pe, g_free, n)
                main(GB, 0)
                if not first:
                    pe.wait_ge(staged, n + 1)
                    soft(GB, 0).then_inc(g_ok, 1)
                wait(pe, us_free, n)
                main(UB, P)
                if first:
                    pe.wait_ge(staged, n + 1)
                    soft(GB, 0).then_inc(g_ok, 1)
                soft(UB, P).then_inc(u_ok, 1)
                r0 = half * E
                mm(SB_[:], mask_st[r0:r0 + E, half, :], flatT[r0:r0 + E, :], start=True, stop=True).then_inc(gu_used, 1)

            def down(t, ph, j, half, start, stop):
                n = (t * 2 + ph) * CH + j * 2 + half
                pe.wait_ge(d_lo_ok, n + 1 + CREDIT)
                pe.wait_ge(a_lo_ok, n + 1)
                for i in range(NT):
                    c = slice(i * P, (i + 1) * P)
                    last = three(YB[i][:], (a_hi[:, half, c], a_lo[:, half, c]), (d_hi[:, half, :], d_lo[:, half, :]), start, stop)
                return last.then_inc(d_used, 1)

            def ffn(t, ph, first):
                r, p = t * 3 + 2 * ph, t * 2 + ph
                ln(r)
                router(r, p)
                gu(t, ph, 0, 0, first)
                for i in range(3):
                    pe.wait_ge(route_cp, p * 3 + i + 1)

                def pair(j, start):
                    gu(t, ph, j, 1, first)
                    down(t, ph, j, 0, start, False)
                    gu(t, ph, j + 1, 0, first)
                    down(t, ph, j, 1, False, False)
                pair(0, True)
                with pe.Fori(1, HALF - 1) as j:
                    pair(j, False)
                gu(t, ph, HALF - 1, 1, first)
                down(t, ph, HALF - 1, 0, False, False)
                down(t, ph, HALF - 1, 1, False, True)

            def attn(t):
                s0 = t * A_STEPS
                r = t * 3 + 1
                ln(r)
                pe.wait_ge(x_lo_ok, (r + 1) * NT)
                for k in range(KC):
                    last = three(XB[0:LOW, :], (k1_hi[:, k, :], k1_lo[:, k, :]), xk(k), k == 0, k == KC - 1)
                last.then_inc(z1_ok, 1)
                for h in range(H):
                    pe.wait_ge(gu_lo_ok, gu_at(t, GU_AT, h) + 1 + CREDIT)
                    hi, lo = (v[:, h % 2, :].rearrange("p (k c) -> p k c", k=KC) for v in (gu_hi, gu_lo))
                    if h >= 2:
                        pe.wait_ge(astep, s0 + 7 * (h - 1))
                    if h == 0:
                        pe.wait_ge(z1_cp, t + 1)
                    mm(YB[h % 2][:], gk2_s[:, h * P:(h + 1) * P], z1s[:], start=True, stop=True).then_inc(z_ok, 1)
                    for b, c, done in ((YB[2 + h % 2], 0, q_ok), ((GB, UB)[h % 2], P, gu_used)):
                        for k in range(KC):
                            last = three(b[:], (hi[:, k, c:c + P], lo[:, k, c:c + P]), xk(k), k == 0, k == KC - 1)
                        last.then_inc(done, 1)
                pe.wait_ge(gu_lo_ok, gu_at(t, GU_AT, AT_SLABS) + CREDIT)
                hi, lo = (v[:].rearrange("p s (k c) -> p (s k) c", k=2) for v in (gu_hi, gu_lo))
                for i in range(NT):
                    c = slice(i * P, (i + 1) * P)
                    if i >= 2:
                        pe.wait_ge(v_cp, t * NT + i - 1)
                    for k in range(KC):
                        last = three((SB_, XB)[i % 2][:], (x_hi[:, k, c], x_lo[:, k, c]), (hi[:, k, :], lo[:, k, :]),
                                     k == 0, k == KC - 1)
                        if i == NT - 1 and k == 1:
                            last.then_inc(gu_used, 1)
                    last.then_inc(gu_used if i == NT - 1 else vg_ok, 1)
                for h in range(H):
                    if h == 0:
                        pe.wait_ge(astep, s0 + 7 * H)
                    if h >= 2:
                        pe.wait_ge(k2_cp, t * H + h - 1)
                    for i in range(NT):
                        c = slice(i * P, (i + 1) * P)
                        last = nc.tensor.transpose(YB[h % 2][:, c], k2[:, h, c], ident[:])
                    last.then_inc(k2T_ok, 1)
                    if h >= 2:
                        pe.wait_ge(sc_cp, t * H + h - 1)
                    for i in range(NT):
                        c = slice(i * P, (i + 1) * P)
                        last = mm(YB[2 + h % 2][:, c], kd[:, h, c], qe[:, h, c], start=True, stop=True)
                    last.then_inc(sc_ok, 1)
                pe.wait_ge(v_cp, (t + 1) * NT)
                for h in range(H):
                    pe.wait_ge(k2_cp, t * H + h + 1)
                    for c in range(NCK):
                        rows = slice(c % 2 * CK, (c % 2 + 1) * CK)
                        last = mm(update(h, c), k2t[rows, h, c // 2, :],
                                  vt[rows, c // 2, h * DV:(h + 1) * DV], start=True, stop=True)
                    last.then_inc(upd_ok, 1)
                pe.wait_ge(sc_mask, (t + 1) * H)
                pe.wait_ge(astep, s0 + 7 * H + 1 + NCK * H)
                for i in range(NT):
                    b = (SB_, XB)[i // 2]
                    for h in range(H):
                        col = slice((i % 2) * H * DV + h * DV, (i % 2) * H * DV + (h + 1) * DV)
                        mm(b[:, col], scm[:, h, i, :], vt[:, i, h * DV:(h + 1) * DV], start=True, stop=False,
                           skip_group_check=True)
                        for half in range(2):
                            q0 = i * P + half * CK
                            last = mm(b[half * CK:(half + 1) * CK, col], qe[:, h, q0:q0 + CK], state[:, 2 * i + half, h, :],
                                      start=False, stop=True, skip_group_check=True)
                    if i % 2:
                        last.then_inc(o_ok, 1)
                pe.wait_ge(astep, s0 + A_STEPS)
                for v in range(2):
                    for i in range(NT):
                        c = i * H * DV + v * P
                        last = nc.tensor.transpose(YB[v][:, i * P:(i + 1) * P], o_w[:, c:c + P], ident[:])
                    last.then_inc(ogT_ok, 1)
                pe.wait_ge(og_lo_ok, t * 2 + 2)
                for i in range(NT):
                    c = slice(i * P, (i + 1) * P)
                    for v in range(2):
                        last = three((YB[2], YB[3], GB, UB)[i][:], (og_hi[:, v, c], og_lo[:, v, c]), (wo_hi[:, v, :], wo_lo[:, v, :]),
                                     v == 0, v == 1)
                    last.then_inc(wo_ok, 1)

            def blk(t, first):
                ffn(t, 0, first)
                attn(t)
                ffn(t, 1, False)

            pe.sem_inc(gu_used, CREDIT)
            pe.sem_inc(d_used, CREDIT)
            pe.wait_ge(ld_const, 16 * N_CONST)
            pe.wait_ge(setup_lo, 1)
            pe.wait_ge(perm_ok, 4)
            blk(0, True)
            with pe.Fori(1, BLOCKS) as t:
                blk(t, False)


def kernel(**inputs):
    import concourse.bacc as bacc
    from concourse.bass_utils import run_bass_kernel_spmd as run

    f = {k.replace("L0_", ""): np.ascontiguousarray(v) for k, v in inputs.items()}

    def fold(w):
        return w.reshape(-1, P, w.shape[1]).transpose(1, 0, 2)

    def inner(w):
        return w.reshape(2, HALF, P, KC, P).transpose(0, 1, 4, 3, 2)

    wgu = np.concatenate([inner(f["ffn_gate_proj_w"]), inner(f["ffn_up_proj_w"])], axis=-1).reshape(2, HALF, P, GW)
    wdn = f["ffn_down_proj_w"].transpose(0, 2, 1).reshape(2, HALF, P, D)
    heads = [np.concatenate([fold(f[n][:, h * P:(h + 1) * P]) for n in ("attn_Wq", "attn_Wk")], axis=-1) for h in range(H)]
    vg = fold(np.concatenate([f["attn_Wv"], f["attn_Wg"]], axis=1))
    wat = np.stack([w.reshape(P, GW) for w in heads] + [vg[:, 2 * s:2 * s + 2, :].reshape(P, GW) for s in range(2)])
    inv = f["ffn_inv_map"]
    inv = inv.view(np.int32).reshape(G, GS, -1)[:, :, 0].reshape(E)
    row = np.arange(P)
    col = np.arange(HALF * P)
    arrays = {
        "x": f["attn_x"].reshape(TOK, D),
        "wgu": wgu,
        "wdn": wdn,
        "wat": wat,
        "w_gate": fold(f["ffn_gate_w"].T),
        "w_mup": fold(f["ffn_mask_up_w"].transpose(1, 0, 2).reshape(D, E)),
        "w_gk1": fold(f["attn_Wgk1"]),
        "w_gk2": f["attn_Wgk2"],
        "bgk": f["attn_bgk2"].reshape(H, P).T,
        "wnorm": f["attn_Wnorm"],
        "wo": fold(f["attn_Wo"]),
        "inv": inv,
        "c_id": np.eye(P, dtype=np.float32),
        "c_mask": (col[None, :] // I == (row[:, None] % (E // 2)) // GS).astype(np.float32),
        "c_reset": np.broadcast_to((np.arange(NB) % CK != 0).astype(np.float32), (P, NB)),
        "c_iota": np.arange(E, dtype=np.float32)[:, None],
    }
    nc = bacc.Bacc("TRN2", target_bir_lowering=False, num_devices=1)
    arrays = {k: np.ascontiguousarray(v) for k, v in arrays.items()}
    args = [nc.dram_tensor(k, v.shape, mybir.dt.from_np(v.dtype), kind="ExternalInput").ap() for k, v in arrays.items()]
    out = nc.dram_tensor("out", (TOK, D), F32, kind="ExternalOutput").ap()
    build(nc, *args, out)
    res = run(nc, [arrays], core_ids=[0])
    return res.results[0]["out"].reshape(f["attn_x"].shape)
```

```python
from contextlib import ExitStack

import numpy as np

import concourse.bass as bass
from concourse import mybir

ALU = mybir.AluOpType
ACT = mybir.ActivationFunctionType
AX = mybir.AxisListType
F32 = mybir.dt.float32
F32R = mybir.dt.float32r
I32 = mybir.dt.int32

P = 128
TOK = 2048
SEQ = 1024
D = 512
KC = D // P
NB = 512
BLOCKS = TOK // NB
BPS = SEQ // NB
NT = NB // P
E = 64
G = 8
GS = E // G
I = 352
HALF = G * I // 2 // P
CH = 2 * HALF
GW = 2 * P * KC
TOPK = 8
H = 4
DV = 64
LOW = 16
CK = 64
NCK = NB // CK
EPS = 1e-5
SCALE = float(P) ** -0.5
NORM = 1.0 / 16.0
CREDIT = 2

AT_SLABS = H + 2
GU_BLOCK = 2 * CH + AT_SLABS
GU_AT = CH
GU_F2 = CH + AT_SLABS
R_STEPS = 22


def attention_steps():
    names = [f"min{h}" for h in range(H)] + ["decay"]
    for h in range(H + 1):
        if h < H:
            names += [f"sum{h}", f"rest{h}"]
        if h:
            names += [f"last{h - 1}", f"kd{h - 1}", f"k2{h - 1}"]
    names += ["state"] + [f"state{c}{h}" for c in range(NCK) for h in range(H)]
    return names + ["gate1", "gate2", "gate3", "gate4", "sq", "norm", "og"]


STEP = {name: i + 1 for i, name in enumerate(attention_steps())}
A_STEPS = len(STEP)
XB_STEPS = 3 * NT


def build(nc, x, wgu, wdn, wat, w_gate, w_mup, w_gk1, w_gk2, bgk, wnorm, wo, inv, c_id, c_mask, c_reset, c_iota, out):
    with ExitStack() as ctx:
        def sb(name, shape, dt=F32):
            return ctx.enter_context(nc.sbuf_tensor(name, shape, dt))

        def sem(name):
            return ctx.enter_context(nc.semaphore(name))

        raw_gu = sb("raw_gu", [P, 2, GW])
        raw_d = sb("raw_d", [P, 2, D])
        gu_hi = sb("gu_hi", [P, 2, GW], F32R)
        gu_lo = sb("gu_lo", [P, 2, GW], F32R)
        d_hi = sb("d_hi", [P, 2, D], F32R)
        d_lo = sb("d_lo", [P, 2, D], F32R)
        x_in = sb("x_in", [P, NT, D])
        x_res = sb("x_res", [P, NT, D])
        xn = sb("xn", [P, NT, D])
        x_hi = sb("x_hi", [P, KC, NB], F32R)
        x_lo = sb("x_lo", [P, KC, NB], F32R)
        m_all = sb("m_all", [P, 2, HALF, 2 * P])
        mask = sb("mask", [P, HALF, P])
        m_st = sb("m_st", [P, 2, 2 * P], F32R)
        mask_st = sb("mask_st", [P, 2, P], F32R)
        softT = sb("softT", [P, 2, NB], F32R)
        flatT = sb("flatT", [P, NB], F32R)
        a_hi = sb("a_hi", [P, 2, NB], F32R)
        a_lo = sb("a_lo", [P, 2, NB], F32R)
        tmp = sb("tmp", [P, 6, NB])
        wo_hi = sb("wo_hi", [P, 2, D], F32R)
        wo_lo = sb("wo_lo", [P, 2, D], F32R)
        gate_s = sb("gate_s", [P, KC, 2 * E], F32R)
        k1_hi = sb("k1_hi", [P, KC, LOW], F32R)
        k1_lo = sb("k1_lo", [P, KC, LOW], F32R)
        mup_hi = sb("mup_hi", [P, 2, KC, P], F32R)
        mup_lo = sb("mup_lo", [P, 2, KC, P], F32R)
        gk2_s = sb("gk2_s", [LOW, D])
        bias = sb("bias", [P, H])
        wn = sb("wn", [P, DV])
        ident = sb("ident", [P, P])
        reset = sb("reset", [P, NB])
        perm = sb("perm", [E, E])
        perm_i = sb("perm_i", [E, E], I32)
        perm_w = sb("perm_w", [E, E])
        iota = sb("iota", [E, 1])
        stats = sb("stats", [P, NT, 6])
        mv = sb("mv", [P, NT, 2])
        ve = sb("ve", [P, NT])
        rstd = sb("rstd", [P, NT])
        mhalf = sb("mhalf", [P, 16])
        r_m = sb("r_m", [P, NT * G])
        r_s = sb("r_s", [P, NT * G])
        top = sb("top", [P, NT, TOPK])
        qe = sb("qe", [P, H, NB])
        k2 = sb("k2", [P, H, NB])
        k2t = sb("k2t", [P, H, NT, P])
        scm = sb("scm", [P, H, NT, P])
        vt = sb("vt", [P, NT, H * DV])
        gt = sb("gt", [P, NT, H * DV])
        dec = sb("dec", [P, H, NCK])
        state = sb("state", [P, NCK, H, DV])
        carry = sb("carry", [P, 2, H * DV])
        ms = sb("ms", [P, 16])
        rr = sb("rr", [P, 16])

        sig, t1, t2 = tmp[:, 0, :], tmp[:, 1, :], tmp[:, 2, :]
        m_raw, m_top = tmp[:, 3, 0:2 * P], tmp[:, 3, 2 * P:4 * P]
        route = tmp[:, 0:3, :].rearrange("p a b -> p (a b)").rearrange("p (t c) -> p t c", t=NT)
        w_eT = tmp[0:E, 3, :]
        kd = xn
        spl = qe
        r_a, r_b, r_c = (k2[:, i, 0:NT * E].rearrange("p (t e) -> p t e", t=NT) for i in range(3))
        z1s = k2t[0:LOW, 0, :, :].rearrange("p t c -> p (t c)")
        o_sb = k2[:, 0:2, :].rearrange("p a b -> p (a b)")
        o_w = k2[:, 2:4, :].rearrange("p a b -> p (a b)")
        o_g = tmp[:, 0:2, :].rearrange("p a b -> p (a b)")
        og_hi, og_lo = a_hi, a_lo
        e_pos, e_neg, e_rest = (tmp[:, 2 * i:2 * i + 2, :] for i in range(3))

        bank = [ctx.enter_context(nc.psum_tensor(f"bank{i}", [P, NB], F32)) for i in range(8)]
        YB, GB, UB, SB_, XB = bank[0:4], bank[4], bank[5], bank[6], bank[7]

        ld_const = sem("ld_const")
        ld_mup = sem("ld_mup")
        ld_x = sem("ld_x")
        st_out = sem("st_out")
        gu_in = [sem(f"gu_in{i}") for i in range(2)]
        d_in = [sem(f"d_in{i}") for i in range(2)]
        gu_hi_ok, gu_lo_ok = sem("gu_hi_ok"), sem("gu_lo_ok")
        d_hi_ok, d_lo_ok = sem("d_hi_ok"), sem("d_lo_ok")
        gu_used, d_used = sem("gu_used"), sem("d_used")
        pool_init, carry_zero = sem("pool_init"), sem("carry_zero")
        setup_hi, setup_lo = sem("setup_hi"), sem("setup_lo")
        perm_ok = sem("perm_ok")
        stats_ok, mv_ok, rstd_ok, xn_ok = sem("stats_ok"), sem("mv_ok"), sem("rstd_ok"), sem("xn_ok")
        ve_ok = sem("ve_ok")
        xT_ok, x_hi_ok, x_lo_ok = sem("xT_ok"), sem("x_hi_ok"), sem("x_lo_ok")
        logit_ok, logit_cp, exp_ok, wT_ok, wT_cp, flat_ok, sexp_ok, routeT_ok, route_cp = (
            sem(n) for n in ("logit_ok", "logit_cp", "exp_ok", "wT_ok", "wT_cp", "flat_ok", "sexp_ok", "routeT_ok", "route_cp"))
        rstep = sem("rstep")
        m_mm, m_masked, m_top_ok, m_ok, staged = (sem(n) for n in ("m_mm", "m_masked", "m_top_ok", "m_ok", "staged"))
        g_ok, u_ok, g_free, gu_prod, us_free, a_hi_ok, a_lo_ok = (
            sem(n) for n in ("g_ok", "u_ok", "g_free", "gu_prod", "us_free", "a_hi_ok", "a_lo_ok"))
        x_ok = sem("x_ok")
        z1_ok, z1_cp, z_ok, q_ok, lsp_a, lsp_e, lsp_ok, eb_ok, enb_ok, ed_ok = (
            sem(n) for n in ("z1_ok", "z1_cp", "z_ok", "q_ok", "lsp_a", "lsp_e", "lsp_ok", "eb_ok", "enb_ok", "ed_ok"))
        astep = sem("astep")
        vg_ok, v_cp, k2T_ok, k2_cp, sc_ok, sc_cp, sc_mask, upd_ok, o_ok, o_cp, rms_v, rms_ok, sg_ok = (
            sem(n) for n in ("vg_ok", "v_cp", "k2T_ok", "k2_cp", "sc_ok", "sc_cp", "sc_mask", "upd_ok", "o_ok", "o_cp", "rms_v", "rms_ok", "sg_ok"))
        waited = sem("waited")
        ogT_ok, og_hi_ok, og_lo_ok, wo_ok = (sem(n) for n in ("ogT_ok", "og_hi_ok", "og_lo_ok", "wo_ok"))

        x_t = x.rearrange("(b t p) d -> b p t d", p=P, t=NT)
        out_t = out.rearrange("(b t p) d -> b p t d", p=P, t=NT)
        N_CONST = 10

        def wait(eng, s, v):
            if not (isinstance(v, int) and v <= 0):
                eng.wait_ge(s, v)

        def mup_copies(half):
            m = k2[:, 1, 0:KC * E].rearrange("p (k h e) -> p k h e", k=KC, h=2)[:, :, half, :]
            return m.unsqueeze(2).broadcast_to([P, KC, 4, E // 2])

        QK = ((GB, UB), (SB_, XB), (YB[0], YB[1]), (YB[2], YB[3]))
        TB = (GB, UB, SB_, XB)

        def astep_at(t, name):
            return t * A_STEPS + STEP[name]

        def update(h, c):
            col = (h % 2) * NB // 2 + (c // 2) * DV
            return ((GB, UB), (SB_, XB))[h // 2][c % 2][:, col:col + DV]

        def settled(eng):
            eng.sem_inc(waited, 1)

        def gu_at(t, off, i):
            return t * GU_BLOCK + off + i

        block = ctx.enter_context(nc.Block())

        @block.sync
        def _(sp):
            def slab(t, off, i, half, src):
                sp.wait_ge(gu_lo_ok, gu_at(t, off, i) + 1)
                sp.dma_start(raw_gu[:, half, :], src).then_inc(gu_in[half], 16)

            def dslab(n, half, src):
                sp.wait_ge(d_lo_ok, n + 1)
                sp.dma_start(raw_d[:, half, :], src).then_inc(d_in[half], 16)

            def ffn(t, ph):
                off = GU_F2 if ph else 0
                with sp.Fori(0, HALF) as j:
                    for half in range(2):
                        slab(t, off, j * 2 + half, half, wgu[half, j])
                        dslab((t * 2 + ph) * CH + j * 2 + half, half, wdn[half, j])

            def attn(t):
                for s in range(AT_SLABS):
                    slab(t, GU_AT, s, s % 2, wat[s])

            def blk(t, more):
                ffn(t, 0)
                attn(t)
                if more:
                    sp.wait_ge(x_ok, t * XB_STEPS + NT)
                    sp.dma_start(x_in[:], x_t[t + 1]).then_inc(ld_x, 16)
                ffn(t, 1)

            sp.dma_start(x_in[:], x_t[0]).then_inc(ld_x, 16)
            sp.dma_start(ident[:], c_id).then_inc(ld_const, 16)
            sp.dma_start(mask[:].rearrange("p a b -> p (a b)"), c_mask).then_inc(ld_const, 16)
            sp.dma_start(reset[:], c_reset).then_inc(ld_const, 16)
            sp.dma_start(iota[:], c_iota).then_inc(ld_const, 16)
            sp.dma_start(gk2_s[:], w_gk2).then_inc(ld_const, 16)
            sp.dma_start(bias[:], bgk).then_inc(ld_const, 16)
            sp.dma_start(wn[:], wnorm.partition_broadcast(P)).then_inc(ld_const, 16)
            sp.dma_start(perm_i[:], inv.partition_broadcast(E)).then_inc(ld_const, 16)
            sp.dma_start(k2[:, 0, :].rearrange("p (k e) -> p k e", k=KC)[:, :, 0:E], w_gate).then_inc(ld_const, 16)
            sp.dma_start(k2[:, 0, :].rearrange("p (k e) -> p k e", k=KC)[:, :, E:E + LOW], w_gk1).then_inc(ld_const, 16)
            sp.dma_start(k2[:, 1, 0:KC * E].rearrange("p (k e) -> p k e", k=KC), w_mup).then_inc(ld_mup, 16)
            sp.dma_start(k2[:, 2:4, :], wo).then_inc(ld_mup, 16)
            blk(0, True)
            with sp.Fori(1, BLOCKS - 1) as t:
                blk(t, True)
            blk(BLOCKS - 1, False)

        @block.gpsimd
        def _(pool):
            nc.gpsimd.memset(mhalf[:], -0.5).then_inc(pool_init, 1)
            nc.gpsimd.memset(carry[:], 0.0).then_inc(carry_zero, 1)
            nc.gpsimd.memset(scm[:], 0.0).then_inc(pool_init, 1)

            def rstd_of(r):
                for i in range(NT):
                    pool.wait_ge(mv_ok, r * NT + i + 1)
                    settled(pool)
                    nc.gpsimd.tensor_scalar(ve[:, i:i + 1], mv[:, i, 1:2], EPS, None, ALU.add).then_inc(ve_ok, 1)
                    pool.wait_ge(ve_ok, r * NT + i + 1)
                    nc.gpsimd.tensor_tensor(rstd[:, i:i + 1], ve[:, i:i + 1], mhalf[:, 0:1], ALU.pow).then_inc(rstd_ok, 1)

            def stage(t, ph, j, first):
                off = GU_F2 if ph else 0
                for half in range(2):
                    pool.wait_ge(gu_used, gu_at(t, off, j * 2 + half) + 1)
                    if first:
                        pool.wait_ge(m_ok, j * 2 + half + 1)
                    settled(pool)
                    nc.gpsimd.tensor_copy(m_st[:, half, :], m_all[:, half, j, :])
                    nc.gpsimd.tensor_copy(mask_st[:, half, :], mask[:, j, :]).then_inc(staged, 1)

            def ffn(t, ph, first, more=False):
                if ph:
                    rstd_of(t * 3 + 2)
                with pool.Fori(0, HALF - 1) as j:
                    stage(t, ph, j, first)
                if more:
                    rstd_of(t * 3 + 3)
                stage(t, ph, HALF - 1, first)

            def attn(t):
                rstd_of(t * 3 + 1)
                for h in range(H):
                    pool.wait_ge(sc_cp, t * H + h + 1)
                    settled(pool)
                    nc.gpsimd.affine_select(out=scm[:, h, :, :], in_=scm[:, h, :, :], compare_op=ALU.is_ge, fill=0.0,
                                            base=0, pattern=[[0, NT], [1, P]], channel_multiplier=-1).then_inc(sc_mask, 1)
                pool.wait_ge(rms_v, t * 2 + 2)
                nc.gpsimd.tensor_tensor(rr[:], ms[:], mhalf[:], ALU.pow).then_inc(rms_ok, 1)

            def blk(t, first, more):
                ffn(t, 0, first)
                attn(t)
                ffn(t, 1, False, more)
                pool.wait_ge(x_ok, (t + 1) * XB_STEPS)
                pool.dma_start(out_t[t], x_res[:]).then_inc(st_out, 16)

            pool.wait_ge(ld_const, 16 * N_CONST)
            rstd_of(0)
            blk(0, True, True)
            with pool.Fori(1, BLOCKS - 1) as t:
                blk(t, False, True)
            blk(BLOCKS - 1, False, False)
            pool.wait_ge(st_out, 16 * BLOCKS)

        @block.scalar
        def _(act):
            def copy(dst, src):
                return nc.scalar.activation(dst, src, ACT.Copy)

            def gu(t, off, j, half):
                act.wait_ge(gu_in[half], (t * (GU_BLOCK // 2) + off // 2 + j + 1) * 16)
                act.wait_ge(gu_used, gu_at(t, off, j * 2 + half) + 1)
                copy(gu_hi[:, half, :], raw_gu[:, half, :]).then_inc(gu_hi_ok, 1)

            def dn(t, ph, j, half):
                n = (t * 2 + ph) * CH + j * 2 + half
                act.wait_ge(d_in[half], ((t * 2 + ph) * HALF + j + 1) * 16)
                act.wait_ge(d_used, n + 1)
                copy(d_hi[:, half, :], raw_d[:, half, :]).then_inc(d_hi_ok, 1)

            def ln(r):
                for i in range(NT):
                    act.wait_ge(xT_ok, r * NT + i + 1)
                    copy(x_hi[:, :, i * P:(i + 1) * P], TB[i][:].rearrange("p (k c) -> p k c", k=KC)).then_inc(x_hi_ok, 1)

            def router(p):
                act.wait_ge(logit_ok, p + 1)
                copy(r_a[:], YB[0][:].rearrange("p (t c) -> p t c", t=NT)[:, :, 0:E]).then_inc(logit_cp, 1)
                act.wait_ge(rstep, p * R_STEPS + 3)
                nc.scalar.activation(r_b[:], r_b[:], ACT.Exp).then_inc(exp_ok, 1)
                act.wait_ge(wT_ok, p + 1)
                copy(w_eT, XB[0:E, :]).then_inc(wT_cp, 1)
                act.wait_ge(rstep, p * R_STEPS + 14)
                nc.scalar.activation(r_b[:], r_b[:], ACT.Exp).then_inc(sexp_ok, 1)
                for i in range(3):
                    act.wait_ge(routeT_ok, p * 3 + i + 1)
                    dst = softT[:, i, :] if i < 2 else flatT[:]
                    copy(dst, YB[i + 1][:]).then_inc(route_cp, 1)

            def chunk(t, ph, j, half, last, first):
                off = GU_F2 if ph else 0
                n = (t * 2 + ph) * CH + j * 2 + half
                if half == 0:
                    gu(t, off, j, 1)
                elif not last:
                    gu(t, off, j + 1, 0)
                dn(t, ph, j, half)
                if first:
                    act.wait_ge(m_masked, n + 1)
                    copy(m_top.bitcast(F32R), m_raw).then_inc(m_top_ok, 1)
                act.wait_ge(g_ok, n + 1)
                act.wait_ge(gu_prod, n + 1)
                nc.scalar.activation(sig, GB[:], ACT.Silu).then_inc(g_free, 1)
                act.wait_ge(us_free, n + 1)
                act.wait_ge(d_used, n + 1)
                copy(a_hi[:, half, :], t2).then_inc(a_hi_ok, 1)

            def ffn(t, ph, first, more=False):
                gu(t, GU_F2 if ph else 0, 0, 0)
                if ph:
                    ln(t * 3 + 2)
                router(t * 2 + ph)
                for half in range(2):
                    chunk(t, ph, 0, half, False, first)
                with act.Fori(1, HALF - 1) as j:
                    for half in range(2):
                        chunk(t, ph, j, half, False, first)
                for half in range(2):
                    chunk(t, ph, HALF - 1, half, True, first)
                if more:
                    ln(t * 3 + 3)

            def attn(t):
                for s in range(2):
                    gu(t, GU_AT, 0, s)
                ln(t * 3 + 1)
                act.wait_ge(z1_ok, t + 1)
                copy(z1s[:], XB[0:LOW, :]).then_inc(z1_cp, 1)
                for h in range(H):
                    act.wait_ge(astep, astep_at(t, f"min{h}"))
                    last = nc.scalar.activation(spl[:, h, :], YB[h][:], ACT.Abs, bias=bias[:, h:h + 1])
                last.then_inc(lsp_a, 1)
                act.wait_ge(lsp_a, t + 1)
                nc.scalar.activation(spl[:], spl[:], ACT.Exp, scale=-1.0).then_inc(lsp_e, 1)
                act.wait_ge(lsp_e, t + 1)
                nc.scalar.activation(spl[:], spl[:], ACT.Ln, bias=1.0).then_inc(lsp_ok, 1)
                for h in range(H):
                    act.wait_ge(astep, astep_at(t, f"sum{h}"))
                    nc.scalar.activation(e_pos[:, h % 2, :], kd[:, h, :], ACT.Exp, scale=NORM).then_inc(eb_ok, 1)
                    nc.scalar.activation(e_neg[:, h % 2, :], kd[:, h, :], ACT.Exp, scale=-NORM).then_inc(enb_ok, 1)
                    act.wait_ge(astep, astep_at(t, f"rest{h}"))
                    nc.scalar.activation(e_rest[:, h % 2, :], e_rest[:, h % 2, :], ACT.Exp, scale=NORM).then_inc(ed_ok, 1)
                    gu(t, GU_AT, h // 2 + 1, h % 2)
                for i in range(NT):
                    if i < NT - 1:
                        act.wait_ge(vg_ok, t * (NT - 1) + i + 1)
                    else:
                        act.wait_ge(gu_used, gu_at(t, GU_AT, AT_SLABS) + CREDIT)
                    copy(vt[:, i, :], TB[i][:, 0:H * DV])
                    copy(gt[:, i, :], TB[i][:, H * DV:]).then_inc(v_cp, 1)
                act.wait_ge(v_cp, (t + 1) * NT)
                act.wait_ge(astep, astep_at(t, f"k2{H - 1}"))
                nc.scalar.activation(o_g, gt[:].rearrange("p t c -> p (t c)"), ACT.Exp, scale=-1.0).then_inc(sg_ok, 1)
                for h in range(H):
                    act.wait_ge(k2T_ok, t * H + h + 1)
                    copy(k2t[:, h, :, :], YB[h % 2][:].rearrange("p (t c) -> p t c", t=NT)).then_inc(k2_cp, 1)
                    act.wait_ge(sc_ok, t * H + h + 1)
                    if h == 0:
                        act.wait_ge(pool_init, 2)
                    b = YB[2 + h % 2][:].rearrange("p (t c) -> p t c", t=NT)
                    copy(scm[0:CK, h, :, 0:CK], b[0:CK, :, 0:CK])
                    copy(scm[CK:P, h, :, CK:P], b[CK:P, :, CK:P]).then_inc(sc_cp, 1)
                for i in range(2):
                    act.wait_ge(o_ok, t * 2 + i + 1)
                    copy(o_sb[:, i * NB:(i + 1) * NB], (SB_, XB)[i][:]).then_inc(o_cp, 1)
                for i in range(2):
                    act.wait_ge(ogT_ok, t * 2 + i + 1)
                    copy(og_hi[:, i, :], (GB, UB)[i][:]).then_inc(og_hi_ok, 1)

            def blk(t, first, more):
                ffn(t, 0, first)
                attn(t)
                ffn(t, 1, False, more)

            act.wait_ge(ld_const, 16 * N_CONST)
            raw = k2[:, 0, :].rearrange("p (k e) -> p k e", k=KC)
            copy(gate_s[:, :, 0:E], raw[:, :, 0:E])
            copy(k1_hi[:], raw[:, :, E:E + LOW])
            act.wait_ge(ld_mup, 32)
            for half in range(2):
                copy(mup_hi[:, half, :, :].rearrange("p k (r e) -> p k r e", r=4), mup_copies(half))
            copy(wo_hi[:], k2[:, 2:4, :]).then_inc(setup_hi, 1)
            ln(0)
            blk(0, True, True)
            with act.Fori(1, BLOCKS - 1) as t:
                blk(t, False, True)
            blk(BLOCKS - 1, False, False)

        @block.vector
        def _(dve):
            def tt(dst, a, b, op):
                return nc.vector.tensor_tensor(dst, a, b, op)

            def gu(t, off, j, half):
                dve.wait_ge(gu_hi_ok, gu_at(t, off, j * 2 + half) + 1)
                tt(gu_lo[:, half, :], raw_gu[:, half, :], gu_hi[:, half, :].bitcast(F32), ALU.subtract).then_inc(gu_lo_ok, 1)

            def dn(t, ph, j, half):
                dve.wait_ge(d_hi_ok, (t * 2 + ph) * CH + j * 2 + half + 1)
                tt(d_lo[:, half, :], raw_d[:, half, :], d_hi[:, half, :].bitcast(F32), ALU.subtract).then_inc(d_lo_ok, 1)

            def stats_of(r, i, src):
                nc.vector.bn_stats(stats[:, i, :], src[:, i, :]).then_inc(stats_ok, 1)
                dve.wait_ge(stats_ok, r * NT + i + 1)
                settled(dve)
                nc.vector.bn_aggr(mv[:, i, :], stats[:, i, :]).then_inc(mv_ok, 1)

            def norm(r, i, src):
                dve.wait_ge(mv_ok, r * NT + i + 1)
                dve.wait_ge(rstd_ok, r * NT + i + 1)
                nc.vector.tensor_scalar(xn[:, i, :], src[:, i, :], mv[:, i, 0:1], rstd[:, i:i + 1],
                                        ALU.subtract, ALU.mult).then_inc(xn_ok, 1)

            def low(r, i):
                dve.wait_ge(x_hi_ok, r * NT + i + 1)
                tt(x_lo[:, :, i * P:(i + 1) * P], TB[i][:].rearrange("p (k c) -> p k c", k=KC),
                   x_hi[:, :, i * P:(i + 1) * P].bitcast(F32), ALU.subtract).then_inc(x_lo_ok, 1)

            def ln_in(t):
                dve.wait_ge(ld_x, (t + 1) * 16)
                for i in range(NT):
                    stats_of(t * 3, i, x_in)
                for i in range(NT):
                    norm(t * 3, i, x_in)

            def ln_res(r, residual):
                for i in range(NT + 2):
                    if i < NT:
                        residual(i)
                        stats_of(r, i, x_res)
                    if 1 <= i <= NT:
                        norm(r, i - 1, x_res)
                    if i >= 2:
                        low(r, i - 2)

            def res_ffn(t, ph):
                src = x_res if ph else x_in

                def residual(i):
                    if i == 0:
                        dve.wait_ge(d_used, (t * 2 + ph + 1) * CH + CREDIT)
                        if not ph:
                            wait(dve, st_out, t * 16)
                    nc.vector.scalar_tensor_tensor(x_res[:, i, :], YB[i][:], 0.5, src[:, i, :], ALU.mult,
                                                   ALU.add).then_inc(x_ok, 1)
                    dve.wait_ge(x_ok, t * XB_STEPS + 2 * NT * ph + i + 1)
                return residual

            def res_attn(t):
                def residual(i):
                    dve.wait_ge(wo_ok, t * NT + i + 1)
                    tt(x_res[:, i, :], YB[i][:], x_res[:, i, :], ALU.add).then_inc(x_ok, 1)
                    dve.wait_ge(x_ok, t * XB_STEPS + NT + i + 1)
                return residual

            def chain(s, base):
                n = [0]

                def step(ins, alone=False):
                    n[0] += 1
                    ins.then_inc(s, 1)
                    dve.wait_ge(s, base + n[0])
                    if alone:
                        settled(dve)
                return step, n

            def bcast(ap, n):
                return ap.unsqueeze(len(ap.shape)).broadcast_to(list(ap.shape) + [n])

            def router(p):
                step, n = chain(rstep, p * R_STEPS)
                r_g = [v[:].rearrange("p t (g s) -> p (t g) s", g=G) for v in (r_a, r_b, r_c)]
                mx, sm = r_m[:, 0:NT], r_s[:, 0:NT]
                dve.wait_ge(logit_cp, p + 1)
                step(tt(r_a[:], YB[0][:].rearrange("p (t c) -> p t c", t=NT)[:, :, E:2 * E], r_a[:], ALU.add))
                step(nc.vector.tensor_reduce(mx, r_a[:], AX.X, ALU.max))
                step(tt(r_b[:], r_a[:], bcast(mx, E), ALU.subtract))
                dve.wait_ge(exp_ok, p + 1)
                step(nc.vector.tensor_reduce(sm, r_b[:], AX.X, ALU.add))
                step(nc.vector.reciprocal(sm, sm))
                step(tt(r_a[:], r_b[:], bcast(sm, E), ALU.mult), True)
                for i in range(NT):
                    last = nc.vector.max(top[:, i, :], r_a[:, i, :])
                step(last, True)
                for i in range(NT):
                    last = nc.vector.match_replace(r_b[:, i, :], top[:, i, :], r_a[:, i, :], 0.0)
                step(last)
                step(tt(r_c[:], r_a[:], r_b[:], ALU.subtract))
                dve.wait_ge(flat_ok, p + 1)
                step(nc.vector.tensor_copy(r_c[:], SB_[:, 0:NT * E].rearrange("p (t e) -> p t e", t=NT)))
                step(nc.vector.tensor_scalar(r_a[:], r_c[:], 0.0, -1e9, ALU.is_equal, ALU.mult))
                step(tt(r_a[:], r_a[:], r_c[:], ALU.add))
                step(nc.vector.tensor_reduce(r_m[:], r_g[0], AX.X, ALU.max))
                step(tt(r_g[1], r_g[0], bcast(r_m[:], GS), ALU.subtract))
                dve.wait_ge(sexp_ok, p + 1)
                step(nc.vector.tensor_reduce(r_s[:], r_g[1], AX.X, ALU.add))
                step(nc.vector.reciprocal(r_s[:], r_s[:]))
                step(tt(r_g[0], r_g[1], bcast(r_s[:], GS), ALU.mult))
                HE = E // 2
                soft = r_a[:].rearrange("p t (h e) -> p t h e", h=2)
                flat = r_c[:].rearrange("p t (h e) -> p t h e", h=2)
                rs = route[:, :, 0:2 * P].rearrange("p t (h c) -> p t h c", h=2)
                rf = route[:, :, 2 * P:3 * P].rearrange("p t (h c) -> p t h c", h=2)
                step(nc.vector.tensor_copy(rs[:, :, :, 0:HE].bitcast(F32R), soft))
                step(tt(rs[:, :, :, HE:2 * HE], soft, rs[:, :, :, 0:HE], ALU.subtract))
                step(nc.vector.tensor_copy(rs[:, :, :, 2 * HE:4 * HE], rs[:, :, :, 0:2 * HE]))
                step(nc.vector.tensor_copy(rf[:, :, :, 0:HE].bitcast(F32R), flat))
                step(tt(rf[:, :, :, HE:2 * HE], flat, rf[:, :, :, 0:HE], ALU.subtract), True)
                assert n[0] == R_STEPS, n

            def chunk(t, ph, j, half, last, first):
                off = GU_F2 if ph else 0
                n = (t * 2 + ph) * CH + j * 2 + half
                if half == 0:
                    gu(t, off, j, 1)
                elif not last:
                    gu(t, off, j + 1, 0)
                dn(t, ph, j, half)
                if first:
                    dve.wait_ge(m_mm, n + 1)
                    mb = mask[:, j, :].unsqueeze(1).broadcast_to([P, 2, P])
                    tt(m_raw.rearrange("p (a c) -> p a c", a=2), XB[:, 0:2 * P].rearrange("p (a c) -> p a c", a=2),
                       mb, ALU.mult).then_inc(m_masked, 1)
                    dve.wait_ge(m_top_ok, n + 1)
                    nc.vector.tensor_copy(m_all[0:E, half, j, :], m_top[0:E, :])
                    tt(m_all[E:P, half, j, :], m_raw[E:P, :], m_top[E:P, :], ALU.subtract).then_inc(m_ok, 1)
                dve.wait_ge(g_free, n + 1)
                dve.wait_ge(u_ok, n + 1)
                tt(t1, UB[:], sig, ALU.mult).then_inc(gu_prod, 1)
                dve.wait_ge(gu_prod, n + 2)
                dve.wait_ge(gu_used, gu_at(t, off, j * 2 + half) + 1 + CREDIT)
                tt(t2, SB_[:], t1, ALU.mult).then_inc(us_free, 1)
                dve.wait_ge(us_free, n + 1)
                dve.wait_ge(a_hi_ok, n + 1)
                tt(a_lo[:, half, :], t2, a_hi[:, half, :].bitcast(F32), ALU.subtract).then_inc(a_lo_ok, 1)

            def ffn(t, ph, first, more=False):
                gu(t, GU_F2 if ph else 0, 0, 0)
                if ph:
                    ln_res(t * 3 + 2, res_attn(t))
                router(t * 2 + ph)
                with dve.Fori(0, HALF - 1) as j:
                    for half in range(2):
                        chunk(t, ph, j, half, False, first)
                if more:
                    ln_in(t + 1)
                for half in range(2):
                    chunk(t, ph, HALF - 1, half, True, first)
                if more:
                    for i in range(NT):
                        low(t * 3 + 3, i)
                if ph:
                    residual = res_ffn(t, ph)
                    for i in range(NT):
                        residual(i)

            def attn(t):
                for s in range(2):
                    gu(t, GU_AT, 0, s)
                ln_res(t * 3 + 1, res_ffn(t, 0))
                done, n = chain(astep, t * A_STEPS)

                def step(name, ins):
                    assert STEP[name] == n[0] + 1, name
                    done(ins)
                for h in range(H):
                    dve.wait_ge(z_ok, t * H + h + 1)
                    step(f"min{h}", nc.vector.tensor_scalar(k2[:, h, :], YB[h][:], bias[:, h:h + 1], 0.0, ALU.add, ALU.min))
                dve.wait_ge(lsp_ok, t + 1)
                step("decay", tt(k2[:], k2[:], spl[:], ALU.subtract))
                for h in range(H + 1):
                    if h < H:
                        step(f"sum{h}", nc.vector.tensor_tensor_scan(kd[:, h, :], reset[:], k2[:, h, :], 0.0, ALU.mult, ALU.add))
                        b3 = kd[:, h, :].rearrange("p (c s) -> p c s", s=CK)
                        step(f"rest{h}", tt(e_rest[:, h % 2, :].rearrange("p (c s) -> p c s", s=CK),
                                            b3[:, :, CK - 1:CK].broadcast_to([P, NCK, CK]), b3, ALU.subtract))
                    if h:
                        g = h - 1
                        qb, kb = QK[g]
                        ep = e_pos[:, g % 2, :]
                        dve.wait_ge(q_ok, t * H + g + 1)
                        dve.wait_ge(eb_ok, t * H + g + 1)
                        nc.vector.scalar_tensor_tensor(qe[:, g, :], qb[:], SCALE, ep, ALU.mult, ALU.mult)
                        step(f"last{g}", nc.vector.tensor_copy(dec[:, g, :], ep.rearrange("p (c s) -> p c s", s=CK)[:, :, CK - 1]))
                        dve.wait_ge(gu_used, gu_at(t, GU_AT, g) + 1 + CREDIT)
                        dve.wait_ge(enb_ok, t * H + g + 1)
                        step(f"kd{g}", tt(kd[:, g, :], kb[:], e_neg[:, g % 2, :], ALU.mult))
                        dve.wait_ge(ed_ok, t * H + g + 1)
                        step(f"k2{g}", tt(k2[:, g, :], kb[:], e_rest[:, g % 2, :], ALU.mult))
                        gu(t, GU_AT, g // 2 + 1, g % 2)
                if isinstance(t, int) and t == 0:
                    dve.wait_ge(carry_zero, 1)
                step("state", nc.vector.tensor_copy(state[:, 0, :, :].rearrange("p h v -> p (h v)"), carry[:, t % BPS, :]))
                dve.wait_ge(upd_ok, (t + 1) * H)
                for c in range(NCK):
                    for h in range(H):
                        new = state[:, c + 1, h, :] if c + 1 < NCK else carry[:, 1, h * DV:(h + 1) * DV]
                        if c:
                            dve.wait_ge(astep, astep_at(t, f"state{c - 1}{h}"))
                        assert STEP[f"state{c}{h}"] == n[0] + 1
                        n[0] += 1
                        nc.vector.scalar_tensor_tensor(new, state[:, c, h, :], dec[:, h, c:c + 1], update(h, c),
                                                       ALU.mult, ALU.add).then_inc(astep, 1)
                o3, w3 = (v.rearrange("p (a v) -> p a v", v=DV) for v in (o_sb, o_w))
                g1 = gt[:].rearrange("p t c -> p (t c)")
                dve.wait_ge(sg_ok, t + 1)
                step("gate1", nc.vector.tensor_scalar(o_g, o_g, 1.0, None, ALU.add))
                step("gate2", nc.vector.reciprocal(o_g, o_g))
                step("gate3", tt(o_g, o_g, g1, ALU.mult))
                step("gate4", tt(o_g.rearrange("p (a v) -> p a v", v=DV), o_g.rearrange("p (a v) -> p a v", v=DV),
                                 wn[:].unsqueeze(1).broadcast_to([P, 16, DV]), ALU.mult))
                dve.wait_ge(o_cp, t * 2 + 2)
                step("sq", tt(o_w, o_sb, o_sb, ALU.mult))
                nc.vector.tensor_reduce(ms[:], w3, AX.X, ALU.add).then_inc(rms_v, 1)
                dve.wait_ge(rms_v, t * 2 + 1)
                nc.vector.tensor_scalar(ms[:], ms[:], 1.0 / DV, EPS, ALU.mult, ALU.add).then_inc(rms_v, 1)
                dve.wait_ge(rms_ok, t + 1)
                step("norm", tt(w3, o3, bcast(rr[:], DV), ALU.mult))
                step("og", tt(o_w, o_w, o_g, ALU.mult))
                for i in range(2):
                    dve.wait_ge(og_hi_ok, t * 2 + i + 1)
                    tt(og_lo[:, i, :], (GB, UB)[i][:], og_hi[:, i, :].bitcast(F32), ALU.subtract).then_inc(og_lo_ok, 1)
                assert n[0] == A_STEPS, n

            def blk(t, first, more):
                ffn(t, 0, first)
                attn(t)
                ffn(t, 1, False, more)

            dve.sem_inc(gu_lo_ok, CREDIT)
            dve.sem_inc(d_lo_ok, CREDIT)
            dve.sem_inc(gu_prod, 1)
            dve.wait_ge(ld_const, 16 * N_CONST)
            nc.vector.tensor_copy(perm_w[:], perm_i[:]).then_inc(perm_ok, 1)
            dve.wait_ge(perm_ok, 1)
            nc.vector.tensor_scalar(perm[:], perm_w[:], 0.0, float(E), ALU.is_lt, ALU.mult).then_inc(perm_ok, 1)
            dve.wait_ge(perm_ok, 2)
            tt(perm[:], perm[:], perm_w[:], ALU.add).then_inc(perm_ok, 1)
            dve.wait_ge(perm_ok, 3)
            nc.vector.tensor_scalar(perm[:], perm[:], iota[:, 0:1], None, ALU.is_equal).then_inc(perm_ok, 1)
            dve.wait_ge(setup_hi, 1)
            raw = k2[:, 0, :].rearrange("p (k e) -> p k e", k=KC)
            tt(gate_s[:, :, E:2 * E], raw[:, :, 0:E], gate_s[:, :, 0:E].bitcast(F32), ALU.subtract)
            tt(k1_lo[:], raw[:, :, E:E + LOW], k1_hi[:].bitcast(F32), ALU.subtract)
            for half in range(2):
                tt(mup_lo[:, half, :, :].rearrange("p k (r e) -> p k r e", r=4), mup_copies(half),
                   mup_hi[:, half, :, :].bitcast(F32).rearrange("p k (r e) -> p k r e", r=4), ALU.subtract)
            tt(wo_lo[:], k2[:, 2:4, :], wo_hi[:].bitcast(F32), ALU.subtract).then_inc(setup_lo, 1)
            ln_in(0)
            for i in range(NT):
                low(0, i)
            blk(0, True, True)
            with dve.Fori(1, BLOCKS - 1) as t:
                blk(t, False, True)
            blk(BLOCKS - 1, False, False)

        @block.tensor
        def _(pe):
            mm = nc.tensor.matmul

            def three(dst, w, xs, start, stop):
                (wh, wl), (xh, xl) = w, xs
                mm(dst, wh, xh, start=start, stop=False)
                mm(dst, wl, xh, start=False, stop=False)
                return mm(dst, wh, xl, start=False, stop=stop)

            def ln(r):
                for i in range(NT):
                    pe.wait_ge(xn_ok, r * NT + i + 1)
                    for k in range(KC):
                        last = nc.tensor.transpose(TB[i][:, k * P:(k + 1) * P], xn[:, i, k * P:(k + 1) * P], ident[:])
                    last.then_inc(xT_ok, 1)

            def logits(t, ph):
                r, p = t * 3 + 2 * ph, t * 2 + ph
                wait(pe, x_ok, t * XB_STEPS + (NT + 1 if ph else 1 - NT))
                for i in range(NT):
                    pe.wait_ge(x_lo_ok, r * NT + i + 1)
                    for k in range(KC):
                        for part in (x_hi, x_lo):
                            last = mm(YB[0][:, i * P:(i + 1) * P], part[:, k, i * P:(i + 1) * P], gate_s[:, k, :],
                                      start=(k == 0 and part is x_hi), stop=(k == KC - 1 and part is x_lo))
                last.then_inc(logit_ok, 1)

            def route_rows(p):
                pe.wait_ge(rstep, p * R_STEPS + 9)
                settled(pe)
                for i in range(NT):
                    last = nc.tensor.transpose(XB[0:E, i * P:(i + 1) * P], r_c[:, i, :], ident[:])
                last.then_inc(wT_ok, 1)
                pe.wait_ge(wT_cp, p + 1)
                for i in range(NT):
                    last = mm(SB_[:, i * E:(i + 1) * E], w_eT[:, i * P:(i + 1) * P], perm[:], start=True, stop=True)
                last.then_inc(flat_ok, 1)
                pe.wait_ge(rstep, p * R_STEPS + R_STEPS)
                for s in range(3):
                    for i in range(NT):
                        last = nc.tensor.transpose(YB[s + 1][:, i * P:(i + 1) * P], route[:, i, s * P:(s + 1) * P], ident[:])
                    last.then_inc(routeT_ok, 1)
                for i in range(3):
                    pe.wait_ge(route_cp, p * 3 + i + 1)

            def xk(k):
                return x_hi[:, k, :], x_lo[:, k, :]

            def gu(t, ph, j, half, first, between=None):
                off = GU_F2 if ph else 0
                n = (t * 2 + ph) * CH + j * 2 + half
                pe.wait_ge(gu_lo_ok, gu_at(t, off, j * 2 + half) + 1 + CREDIT)
                hi, lo = (v[:, half, :].rearrange("p (k c) -> p k c", k=KC) for v in (gu_hi, gu_lo))

                def masked():
                    wait(pe, m_masked, n)
                    for k in range(KC):
                        mm(XB[:, 0:2 * P], mup_hi[:, half, k, :], hi[:, k, :], start=(k == 0), stop=False)
                        mm(XB[:, 0:2 * P], mup_lo[:, half, k, :], hi[:, k, :], start=False, stop=False)
                        mm(XB[:, 0:2 * P], mup_hi[:, half, k, :], lo[:, k, :], start=False, stop=False)
                        last = mm(XB[:, 0:2 * P], mup_lo[:, half, k, :], lo[:, k, :], start=False, stop=(k == KC - 1))
                    last.then_inc(m_mm, 1)

                def main(b, c):
                    for k in range(KC):
                        three(b[:], (hi[:, k, c:c + P], lo[:, k, c:c + P]), xk(k), k == 0, False)

                def soft(b, c):
                    return mm(b[:], m_st[:, half, c:c + P], softT[:, half, :], start=False, stop=True)

                late = first or between
                if first and not between:
                    masked()
                wait(pe, g_free, n)
                main(GB, 0)
                if not late:
                    pe.wait_ge(staged, n + 1)
                    soft(GB, 0).then_inc(g_ok, 1)
                wait(pe, us_free, n)
                main(UB, P)
                if between:
                    between()
                    if first:
                        masked()
                if late:
                    pe.wait_ge(staged, n + 1)
                    soft(GB, 0).then_inc(g_ok, 1)
                soft(UB, P).then_inc(u_ok, 1)
                r0 = half * E
                mm(SB_[:], mask_st[r0:r0 + E, half, :], flatT[r0:r0 + E, :], start=True, stop=True).then_inc(gu_used, 1)

            def down(t, ph, j, half, start, stop):
                n = (t * 2 + ph) * CH + j * 2 + half
                pe.wait_ge(d_lo_ok, n + 1 + CREDIT)
                pe.wait_ge(a_lo_ok, n + 1)
                for i in range(NT):
                    c = slice(i * P, (i + 1) * P)
                    last = three(YB[i][:], (a_hi[:, half, c], a_lo[:, half, c]), (d_hi[:, half, :], d_lo[:, half, :]), start, stop)
                return last.then_inc(d_used, 1)

            def ffn(t, ph, first, more=False):
                if ph:
                    ln(t * 3 + 2)
                logits(t, ph)
                gu(t, ph, 0, 0, first, lambda: route_rows(t * 2 + ph))

                def pair(j, start):
                    gu(t, ph, j, 1, first)
                    down(t, ph, j, 0, start, False)
                    gu(t, ph, j + 1, 0, first)
                    down(t, ph, j, 1, False, False)
                pair(0, True)
                with pe.Fori(1, HALF - 1) as j:
                    pair(j, False)
                gu(t, ph, HALF - 1, 1, first)
                down(t, ph, HALF - 1, 0, False, False)
                if more:
                    pe.wait_ge(us_free, (t * 2 + 2) * CH)
                    ln(t * 3 + 3)
                down(t, ph, HALF - 1, 1, False, True)

            def attn(t):
                r = t * 3 + 1
                ln(r)
                pe.wait_ge(x_lo_ok, (r + 1) * NT)
                for k in range(KC):
                    last = three(XB[0:LOW, :], (k1_hi[:, k, :], k1_lo[:, k, :]), xk(k), k == 0, k == KC - 1)
                last.then_inc(z1_ok, 1)

                def head(h):
                    pe.wait_ge(gu_lo_ok, gu_at(t, GU_AT, h) + 1 + CREDIT)
                    hi, lo = (v[:, h % 2, :].rearrange("p (k c) -> p k c", k=KC) for v in (gu_hi, gu_lo))
                    for b, c, done in ((QK[h][0], 0, q_ok), (QK[h][1], P, gu_used)):
                        for k in range(KC):
                            last = three(b[:], (hi[:, k, c:c + P], lo[:, k, c:c + P]), xk(k), k == 0, k == KC - 1)
                        last.then_inc(done, 1)

                pe.wait_ge(z1_cp, t + 1)
                for h in range(H):
                    mm(YB[h][:], gk2_s[:, h * P:(h + 1) * P], z1s[:], start=True, stop=True).then_inc(z_ok, 1)
                head(0)
                head(1)
                pe.wait_ge(lsp_a, t + 1)
                head(2)
                head(3)
                pe.wait_ge(gu_lo_ok, gu_at(t, GU_AT, AT_SLABS) + CREDIT)
                hi, lo = (v[:].rearrange("p s (k c) -> p (s k) c", k=2) for v in (gu_hi, gu_lo))
                for i in range(NT):
                    c = slice(i * P, (i + 1) * P)
                    if i % 2 == 0:
                        pe.wait_ge(astep, astep_at(t, f"k2{i // 2}"))
                    for k in range(KC):
                        last = three(TB[i][:], (x_hi[:, k, c], x_lo[:, k, c]), (hi[:, k, :], lo[:, k, :]),
                                     k == 0, k == KC - 1)
                        if i == NT - 1 and k == 1:
                            last.then_inc(gu_used, 1)
                    last.then_inc(gu_used if i == NT - 1 else vg_ok, 1)
                for h in range(H):
                    if h == 0:
                        pe.wait_ge(astep, astep_at(t, f"k2{H - 1}"))
                    if h >= 2:
                        pe.wait_ge(k2_cp, t * H + h - 1)
                    for i in range(NT):
                        c = slice(i * P, (i + 1) * P)
                        last = nc.tensor.transpose(YB[h % 2][:, c], k2[:, h, c], ident[:])
                    last.then_inc(k2T_ok, 1)
                    if h >= 2:
                        pe.wait_ge(sc_cp, t * H + h - 1)
                    for i in range(NT):
                        c = slice(i * P, (i + 1) * P)
                        last = mm(YB[2 + h % 2][:, c], kd[:, h, c], qe[:, h, c], start=True, stop=True)
                    last.then_inc(sc_ok, 1)
                pe.wait_ge(v_cp, (t + 1) * NT)
                for h in range(H):
                    pe.wait_ge(k2_cp, t * H + h + 1)
                    for c in range(NCK):
                        rows = slice(c % 2 * CK, (c % 2 + 1) * CK)
                        last = mm(update(h, c), k2t[rows, h, c // 2, :],
                                  vt[rows, c // 2, h * DV:(h + 1) * DV], start=True, stop=True)
                    last.then_inc(upd_ok, 1)
                pe.wait_ge(sc_mask, (t + 1) * H)
                pe.wait_ge(astep, astep_at(t, f"state{NCK - 1}{H - 1}"))
                for i in range(NT):
                    b = (SB_, XB)[i // 2]
                    for h in range(H):
                        col = slice((i % 2) * H * DV + h * DV, (i % 2) * H * DV + (h + 1) * DV)
                        mm(b[:, col], scm[:, h, i, :], vt[:, i, h * DV:(h + 1) * DV], start=True, stop=False,
                           skip_group_check=True)
                        for half in range(2):
                            q0 = i * P + half * CK
                            last = mm(b[half * CK:(half + 1) * CK, col], qe[:, h, q0:q0 + CK], state[:, 2 * i + half, h, :],
                                      start=False, stop=True, skip_group_check=True)
                    if i % 2:
                        last.then_inc(o_ok, 1)
                pe.wait_ge(astep, astep_at(t, "og"))
                for v in range(2):
                    for i in range(NT):
                        c = i * H * DV + v * P
                        last = nc.tensor.transpose((GB, UB)[v][:, i * P:(i + 1) * P], o_w[:, c:c + P], ident[:])
                    last.then_inc(ogT_ok, 1)
                pe.wait_ge(og_lo_ok, t * 2 + 2)
                for i in range(NT):
                    c = slice(i * P, (i + 1) * P)
                    for v in range(2):
                        last = three(YB[i][:], (og_hi[:, v, c], og_lo[:, v, c]), (wo_hi[:, v, :], wo_lo[:, v, :]),
                                     v == 0, v == 1)
                    last.then_inc(wo_ok, 1)

            def blk(t, first, more):
                ffn(t, 0, first)
                attn(t)
                ffn(t, 1, False, more)

            pe.sem_inc(gu_used, CREDIT)
            pe.sem_inc(d_used, CREDIT)
            pe.wait_ge(ld_const, 16 * N_CONST)
            pe.wait_ge(setup_lo, 1)
            pe.wait_ge(perm_ok, 4)
            ln(0)
            blk(0, True, True)
            with pe.Fori(1, BLOCKS - 1) as t:
                blk(t, False, True)
            blk(BLOCKS - 1, False, False)


def kernel(**inputs):
    import concourse.bacc as bacc
    from concourse.bass_utils import run_bass_kernel_spmd as run

    f = {k.replace("L0_", ""): np.ascontiguousarray(v) for k, v in inputs.items()}

    def fold(w):
        return w.reshape(-1, P, w.shape[1]).transpose(1, 0, 2)

    def inner(w):
        return w.reshape(2, HALF, P, KC, P).transpose(0, 1, 4, 3, 2)

    wgu = np.concatenate([inner(f["ffn_gate_proj_w"]), inner(f["ffn_up_proj_w"])], axis=-1).reshape(2, HALF, P, GW)
    wdn = f["ffn_down_proj_w"].transpose(0, 2, 1).reshape(2, HALF, P, D)
    heads = [np.concatenate([fold(f[n][:, h * P:(h + 1) * P]) for n in ("attn_Wq", "attn_Wk")], axis=-1) for h in range(H)]
    vg = fold(np.concatenate([f["attn_Wv"], f["attn_Wg"]], axis=1))
    wat = np.stack([w.reshape(P, GW) for w in heads] + [vg[:, 2 * s:2 * s + 2, :].reshape(P, GW) for s in range(2)])
    inv = f["ffn_inv_map"]
    inv = inv.view(np.int32).reshape(G, GS, -1)[:, :, 0].reshape(E)
    row = np.arange(P)
    col = np.arange(HALF * P)
    arrays = {
        "x": f["attn_x"].reshape(TOK, D),
        "wgu": wgu,
        "wdn": wdn,
        "wat": wat,
        "w_gate": fold(f["ffn_gate_w"].T),
        "w_mup": fold(f["ffn_mask_up_w"].transpose(1, 0, 2).reshape(D, E)),
        "w_gk1": fold(f["attn_Wgk1"]),
        "w_gk2": f["attn_Wgk2"],
        "bgk": f["attn_bgk2"].reshape(H, P).T,
        "wnorm": f["attn_Wnorm"],
        "wo": fold(f["attn_Wo"]),
        "inv": inv,
        "c_id": np.eye(P, dtype=np.float32),
        "c_mask": (col[None, :] // I == (row[:, None] % (E // 2)) // GS).astype(np.float32),
        "c_reset": np.broadcast_to((np.arange(NB) % CK != 0).astype(np.float32), (P, NB)),
        "c_iota": np.arange(E, dtype=np.float32)[:, None],
    }
    nc = bacc.Bacc("TRN2", target_bir_lowering=False, num_devices=1)
    arrays = {k: np.ascontiguousarray(v) for k, v in arrays.items()}
    args = [nc.dram_tensor(k, v.shape, mybir.dt.from_np(v.dtype), kind="ExternalInput").ap() for k, v in arrays.items()]
    out = nc.dram_tensor("out", (TOK, D), F32, kind="ExternalOutput").ap()
    build(nc, *args, out)
    res = run(nc, [arrays], core_ids=[0])
    return res.results[0]["out"].reshape(f["attn_x"].shape)
```
